# Optimizing a Trainium2 kernel written in Bass

```python
import numpy as np
import jax
import jax.numpy as jnp

def _softmax(x, axis=-1):
    return jax.nn.softmax(x, axis=axis)

def _gelu(x):
    return jax.nn.gelu(x, approximate=True)

def _silu(x):
    return jax.nn.silu(x)

def _sigmoid(x):
    return jax.nn.sigmoid(x)

def _layernorm(x, axis=-1, eps=1e-05):
    m = jnp.mean(x, axis=axis, keepdims=True)
    v = jnp.var(x, axis=axis, keepdims=True)
    return (x - m) / jnp.sqrt(v + eps)

def _scatter_add(tgt, idx, src, axis=0):
    return tgt.at[idx].add(src)

def _segment_sum(src, seg, n):
    return jax.ops.segment_sum(src, seg, n)
kernel_name = 'mk_flamingo_gated_d1_seqx_r8_20ba4e'

def setup_inputs(seed: int=0):
    np.random.seed(seed)
    _w = jnp.asarray

    def _rec_inputs():
        import jax
        import jax.numpy as jnp
        _rk = jax.random.key(seed)
        x = -0.0003929 + 0.9999 * jax.random.normal(jax.random.fold_in(_rk, 1), (1, 1024, 128), jnp.float32)
        _lenS = 1024 - jax.random.randint(jax.random.fold_in(_rk, 7), (1,), 0, max(1, 1024 // 4) + 1, jnp.int32)
        _lenS2 = 6404 - jax.random.randint(jax.random.fold_in(_rk, 8), (1,), 0, max(1, 6404 // 4) + 1, jnp.int32)
        _ctx_768P = jax.random.normal(jax.random.fold_in(_rk, 11), (1, 16, 96), jnp.float32)
        _ctx_768c = jax.random.dirichlet(jax.random.fold_in(_rk, 511), 0.3 * jnp.ones((16,), jnp.float32), (1, 6404))
        _ctx_768t = jnp.einsum('bsk,bkd->bsd', _ctx_768c, _ctx_768P)
        _ctx_768t = _ctx_768t * jax.lax.rsqrt(jnp.mean(jnp.square(_ctx_768t)) + 1e-12) * 0.953939
        ctx_768 = -7.36909e-05 + 0.999899 * (_ctx_768t + 0.3 * jax.random.normal(jax.random.fold_in(_rk, 611), (1, 6404, 96), jnp.float32))
        _g = jax.random.normal(jax.random.fold_in(_rk, 9001), (2, 1), jnp.float32)
        _g = jnp.sign(_g) * jnp.maximum(jnp.abs(_g), 1.0) + (_g == 0) * 1.0
        g_xattn = _g[0]
        g_ffn = _g[1]
        return (x, ctx_768, g_xattn, g_ffn)
    x, ctx_768, g_xattn, g_ffn = _rec_inputs()

    def _L0_xattn_setup():
        import jax, jax.numpy as jnp
        import numpy as np
        IMG_DIM, TXT_DIM, HID = (128, 96, 128)
        B, LQ, LK = (8, 256, 256)
        key = jax.random.key(seed)
        ks = jax.random.split(key, 8)
        s_img = 1.0 / np.sqrt(IMG_DIM)
        s_txt = 1.0 / np.sqrt(TXT_DIM)
        return {'image_features': jax.random.normal(ks[0], (B, LQ, IMG_DIM), jnp.float32), 'text_features': jax.random.normal(ks[1], (B, LK, TXT_DIM), jnp.float32), 'Wq': jax.random.uniform(ks[2], (IMG_DIM, HID), jnp.float32, -s_img, s_img), 'bq': jax.random.uniform(ks[3], (HID,), jnp.float32, -s_img, s_img), 'Wk': jax.random.uniform(ks[4], (TXT_DIM, HID), jnp.float32, -s_txt, s_txt), 'bk': jax.random.uniform(ks[5], (HID,), jnp.float32, -s_txt, s_txt), 'Wv': jax.random.uniform(ks[6], (TXT_DIM, HID), jnp.float32, -s_txt, s_txt), 'bv': jax.random.uniform(ks[7], (HID,), jnp.float32, -s_txt, s_txt)}
    _L0_xattn_all = _L0_xattn_setup()
    _L0_xattn_in = {k: v for k, v in _L0_xattn_all.items() if k in ('Wq', 'bq', 'Wk', 'bk', 'Wv', 'bv')}
    del _L0_xattn_all

    def _L0_ffn_setup():
        import jax, jax.numpy as jnp
        import numpy as np
        B, S, D = (4, 256, 128)
        EXP = 4
        H = EXP * D
        E = 8
        TOP_K = 2
        key = jax.random.key(seed)
        ks = jax.random.split(key, 8)
        scale1 = 1.0 / np.sqrt(D)
        scale2 = 1.0 / np.sqrt(H)
        x = jax.random.normal(ks[0], (B, S, D), dtype=jnp.float32)
        W1 = jax.random.uniform(ks[1], (E, D, H), jnp.float32, -scale1, scale1)
        b1 = jax.random.uniform(ks[2], (E, H), jnp.float32, -scale1, scale1)
        W2 = jax.random.uniform(ks[3], (E, H, D), jnp.float32, -scale2, scale2)
        b2 = jax.random.uniform(ks[4], (E, D), jnp.float32, -scale2, scale2)
        Wr = jax.random.uniform(ks[5], (D, E), jnp.float32, -scale1, scale1)
        br = jax.random.uniform(ks[6], (E,), jnp.float32, -scale1, scale1)
        return {'input_emb': x, 'W1': W1, 'b1': b1, 'W2': W2, 'b2': b2, 'Wr': Wr, 'br': br}
    _L0_ffn_all = _L0_ffn_setup()
    _L0_ffn_in = {k: v for k, v in _L0_ffn_all.items() if k in ('W1', 'b1', 'W2', 'b2', 'Wr', 'br')}
    del _L0_ffn_all
    return {'x': x, 'ctx_768': ctx_768, 'g_xattn': g_xattn, 'g_ffn': g_ffn, 'L0_xattn_Wq': _L0_xattn_in['Wq'], 'L0_xattn_bq': _L0_xattn_in['bq'], 'L0_xattn_Wk': _L0_xattn_in['Wk'], 'L0_xattn_bk': _L0_xattn_in['bk'], 'L0_xattn_Wv': _L0_xattn_in['Wv'], 'L0_xattn_bv': _L0_xattn_in['bv'], 'L0_ffn_W1': _L0_ffn_in['W1'], 'L0_ffn_b1': _L0_ffn_in['b1'], 'L0_ffn_W2': _L0_ffn_in['W2'], 'L0_ffn_b2': _L0_ffn_in['b2'], 'L0_ffn_Wr': _L0_ffn_in['Wr'], 'L0_ffn_br': _L0_ffn_in['br']}

def reference(x, ctx_768, g_xattn, g_ffn, L0_xattn_Wq, L0_xattn_bq, L0_xattn_Wk, L0_xattn_bk, L0_xattn_Wv, L0_xattn_bv, L0_ffn_W1, L0_ffn_b1, L0_ffn_W2, L0_ffn_b2, L0_ffn_Wr, L0_ffn_br):
    import jax
    import jax.numpy as jnp

    def _L0_xattn_ref(image_features, text_features, Wq, bq, Wk, bk, Wv, bv):
        import jax, jax.numpy as jnp
        import numpy as np
        IMG_DIM, TXT_DIM, HID = (128, 96, 128)
        B, LQ, LK = (8, 256, 256)
        query = jnp.einsum('bqi,ih->bqh', image_features, Wq) + bq
        key = jnp.einsum('bkt,th->bkh', text_features, Wk) + bk
        value = jnp.einsum('bkt,th->bkh', text_features, Wv) + bv
        scale = 1.0 / jnp.sqrt(jnp.asarray(HID, query.dtype))
        scores = jnp.einsum('bqh,bkh->bqk', query, key) * scale
        weights = jax.nn.softmax(scores, axis=-1)
        attended = jnp.einsum('bqk,bkh->bqh', weights, value)
        return attended

    def _L0_ffn_ref(input_emb, W1, b1, W2, b2, Wr, br):
        import jax, jax.numpy as jnp
        import numpy as np
        B, S, D = (4, 256, 128)
        EXP = 4
        H = EXP * D
        E = 8
        TOP_K = 2
        logits = jnp.einsum('bsd,de->bse', input_emb, Wr) + br
        route_w = jax.nn.softmax(logits, axis=-1)
        _, topk_idx = jax.lax.top_k(route_w, TOP_K)
        mask = jax.nn.one_hot(topk_idx, E, dtype=route_w.dtype).sum(-2)
        routed = route_w * mask
        routed = routed / routed.sum(axis=-1, keepdims=True)
        h = jax.nn.relu(jnp.einsum('bsd,edh->ebsh', input_emb, W1) + b1[:, None, None, :])
        expert_out = jnp.einsum('ebsh,ehd->ebsd', h, W2) + b2[:, None, None, :]
        return jnp.einsum('bse,ebsd->bsd', routed, expert_out)
    x = x + jnp.tanh(g_xattn[0]) * _L0_xattn_ref(_layernorm(x, axis=-1), ctx_768, L0_xattn_Wq, L0_xattn_bq, L0_xattn_Wk, L0_xattn_bk, L0_xattn_Wv, L0_xattn_bv)
    x = x + jnp.tanh(g_ffn[0]) * _L0_ffn_ref(_layernorm(x, axis=-1), L0_ffn_W1, L0_ffn_b1, L0_ffn_W2, L0_ffn_b2, L0_ffn_Wr, L0_ffn_br)
    return x

_drawn_inputs = setup_inputs


def setup_inputs(seed=0):
    import zlib

    import numpy as np

    out = dict(_drawn_inputs(seed))
    spreads = {}
    factors = {'L0_xattn_bq': 8.0, 'L0_xattn_bk': 8.0, 'L0_ffn_b1': 4.13, 'L0_ffn_b2': 3.433}
    for name, (base, spread) in spreads.items():
        noise = np.random.default_rng([zlib.crc32(name.encode()), seed]).standard_normal(out[name].shape)
        drawn = base * np.exp(spread * noise) if base else spread * noise
        out[name] = jnp.asarray(drawn.astype(out[name].dtype))
    for name, factor in factors.items():
        out[name] = (out[name] * factor).astype(out[name].dtype)
    return out
```

```python
from contextlib import ExitStack

import concourse.bass as bass
from concourse import mybir

F32 = mybir.dt.float32
F32R = mybir.dt.float32r
ALU = mybir.AluOpType
ACT = mybir.ActivationFunctionType
AX = mybir.AxisListType

P = 128
BANK = 512
BLOCK_TILES = [2, 3, 3]
NB = len(BLOCK_TILES)
FIRST_TILE = [sum(BLOCK_TILES[:b]) for b in range(NB)]
FFN_ORDER = [1, 0, 2]
TRANSPOSE_GROUP = 8
LAG = 2
P_RING = 3
W_RING = 2
EPS = 1e-5

POST = dict(u_copy=3, project=5, residual=6, normalize=8, turn=10, split=11, logits=13,
            soft1=14, soft2=15, soft3=16, turn_r=18, copy_r=19)


def attention_experts(nc, x, ctx, g_xattn, g_ffn, wq, bq, wk, bk, wv, bv, w1, b1, w2, b2, wr, br, out):
    _, NTOK, D = x.shape
    _, NKEY, C = ctx.shape
    HID = wq.shape[1]
    E, _, H = w1.shape
    NT = NTOK // P
    FULL = NKEY // P
    TAIL = NKEY - FULL * P
    NC = FULL + 1
    CA = C + 1
    NG = -(-NC // TRANSPOSE_GROUP)
    UNITS = -(-NC // 2)
    HC = H // P
    FU = E * HC
    SCALE = float(HID) ** -0.5
    MAXN = max(BLOCK_TILES) * P
    assert D == P and HID == P and sum(BLOCK_TILES) == NT and TAIL > 0 and C == 96

    xv = x.rearrange("a (p t) d -> p (a t) d", t=NT)
    outv = out.rearrange("a (p t) d -> p (a t) d", t=NT)
    ctxv = ctx[0, 0:FULL * P, :].rearrange("(p j) c -> p j c", j=FULL)

    def group_chunks(g):
        return range(g * TRANSPOSE_GROUP, min((g + 1) * TRANSPOSE_GROUP, NC))

    def unit_chunks(i):
        return range(2 * i, min(2 * i + 2, NC))

    def max_slots(b):
        n, wide = BLOCK_TILES[b], NKEY // (2 * BANK)
        last = NKEY - wide * 2 * BANK
        assert last <= BANK
        slots = [((t,), 2 * BANK * w, BANK, w) for w in range(wide) for t in range(n)]
        slots += [(tuple(range(t, min(t + 2, n))), 2 * BANK * wide, last, wide) for t in range(0, n, 2)]
        return slots

    NMAX = NKEY // (2 * BANK) + 1
    SLOTS = [max_slots(b) for b in range(NB)]
    SLOTS_BEFORE = [sum(len(s) for s in SLOTS[:b]) for b in range(NB)]
    FIRST_SLOT_UNIT = 1
    MAX_ROW_UNIT = UNITS - 2

    with ExitStack() as stack:
        def sb(name, shape, dt=F32):
            return stack.enter_context(nc.sbuf_tensor(name, shape, dt))

        def sem(name):
            return stack.enter_context(nc.semaphore(name))

        raw = sb("raw", [P, NC, C])
        ctx_hi = sb("ctx_hi", [P, NC * CA], F32R)
        ctx_lo = sb("ctx_lo", [P, NC * C], F32R)
        ctxT_hi = sb("ctxT_hi", [P, NC * P], F32R)
        ctxT_lo = sb("ctxT_lo", [P, NC * P], F32R)
        ch = ctx_hi[:, :].rearrange("p (j c) -> p j c", c=CA)
        cl = ctx_lo[:, :].rearrange("p (j c) -> p j c", c=C)
        w1_hi = ctxT_hi[:, 0:E * H]
        w1_lo = ctxT_lo[:, 0:E * H]
        w2_hi = ctx_hi[:, 0:E * H].rearrange("p (e c d) -> p e c d", e=E, d=D)
        w2_lo = ctx_lo[:, 0:E * H].rearrange("p (e c d) -> p e c d", e=E, d=D)
        w_raw = sb("w_raw", [P, W_RING, 2, H])

        ident = sb("ident", [P, P])
        wq_sb = sb("wq_sb", [P, HID])
        wk_sb = sb("wk_sb", [CA, HID])
        wkT = sb("wkT", [HID, CA])
        wv_sb = sb("wv_sb", [CA, HID + 1])
        NROW = E * HC + E + 1
        rows = sb("rows", [NROW, P])
        cols = sb("cols", [P, NROW])
        wr_sb = sb("wr_sb", [P, E])
        br_sb = sb("br_sb", [P, E])
        gates = sb("gates", [P, 2])
        tanh_g = sb("tanh_g", [P, 2])
        minus_half = sb("minus_half", [P, NT])
        earlier = sb("earlier", [P, E, E])
        sel = sb("sel", [2 * E, E, P], F32R)

        tok = sb("tok", [P, NT, D])
        norm = sb("norm", [P, NT, D])
        stats = sb("stats", [P, 2, NT, 6])
        mv = sb("mv", [P, 2, NT, 2])
        veps = sb("veps", [P, 2, NT])
        rstd = sb("rstd", [P, 2, NT])
        xT = sb("xT", [P, NTOK])
        qT = sb("qT", [P, MAXN])
        q_f = sb("q_f", [CA, NTOK])
        q_hi = sb("q_hi", [CA, NTOK], F32R)
        q_lo = sb("q_lo", [C, NTOK], F32R)
        pmax = sb("pmax", [P, NT, NMAX])
        nmax = sb("nmax", [P, NT])
        ex = sb("ex", [P, P_RING, 2 * MAXN])
        ex_hi = sb("ex_hi", [P, P_RING, 2 * MAXN], F32R)
        ex_lo = sb("ex_lo", [P, P_RING, 2 * MAXN], F32R)
        u_sb = sb("u_sb", [CA, MAXN])
        rsum = sb("rsum", [P, NT])
        gsum = sb("gsum", [P, NT])
        xT_hi = sb("xT_hi", [P, NTOK], F32R)
        xT_lo = sb("xT_lo", [P, NTOK], F32R)
        lg = sb("lg", [P, NT, E])
        lmax = sb("lmax", [P, NT])
        ld = sb("ld", [P, NT, E])
        le = sb("le", [P, NT, E])
        cmp_gt = sb("cmp_gt", [P, 3, E, E])
        cmp_eq = sb("cmp_eq", [P, 3, E, E])
        rank = sb("rank", [P, NT, E])
        esum = sb("esum", [P, NT])
        einv = sb("einv", [P, NT])
        picked = sb("picked", [P, NT, E])
        psumw = sb("psumw", [P, NT])
        pinv = sb("pinv", [P, NT])
        routed = sb("routed", [P, NT, E])
        r_hi = sb("r_hi", [P, NT, E], F32R)
        r_cat = sb("r_cat", [P, NT, 2 * E])
        rT = sb("rT", [2 * E, NTOK], F32R)
        r_b = sb("r_b", [P, 2, MAXN])
        y_r = sb("y_r", [P, 2, MAXN])
        acc = sb("acc", [P, NTOK])
        result = norm
        sel_f = acc[0:2 * E, :].rearrange("k (e p) -> k e p", e=E)

        ps = stack.enter_context(nc.psum_tensor("ps", [P, 8, BANK], F32))
        SPAIR = [ps[:, 0:2, :], ps[:, 2:4, :]]
        MPAIR = ps[:, 4:6, :]
        UB = [ps[:, 6, :], ps[:, 7, :]]

        small_in, x_in, w_consts_in = sem("small_in"), sem("x_in"), sem("w_consts_in")
        ctx_in = [sem(f"ctx_in{g}") for g in range(NG)]
        w_in = [sem(f"w_in{r}") for r in range(W_RING)]
        out_done = sem("out_done")
        ident_ready, pad_zeroed, ones_ready, sel_ready, pool_step = sem("ident_ready"), sem("pad_zeroed"), sem("ones_ready"), sem("sel_ready"), sem("pool_step")
        small_turned, small_copied, tanh_ready = sem("small_turned"), sem("small_copied"), sem("tanh_ready")
        var_ready, rstd_ready, norm_ready = sem("var_ready"), sem("rstd_ready"), sem("norm_ready")
        x_turned, x_copied = sem("x_turned"), sem("x_copied")
        q_made, q_copied, qk_made, qk_copied, q_lo_ready = sem("q_made"), sem("q_copied"), sem("qk_made"), sem("qk_copied"), sem("q_lo_ready")
        ctx_turned, ctxT_hi_ready, ctxT_lo_ready = sem("ctx_turned"), sem("ctxT_hi_ready"), sem("ctxT_lo_ready")
        ctx_hi_ready, ctx_lo_ready = sem("ctx_hi_ready"), sem("ctx_lo_ready")
        max_scores, max_reduced, nmax_ready, max_row, row_ready = sem("max_scores"), sem("max_reduced"), sem("nmax_ready"), sem("max_row"), sem("row_ready")
        scores_ready, ex_ready, lo_ready, ex_used = sem("scores_ready"), sem("ex_ready"), sem("lo_ready"), sem("ex_used")
        u_copied, projected, resid_ready, logits_ready, soft_in, exp_ready = sem("u_copied"), sem("projected"), sem("resid_ready"), sem("logits_ready"), sem("soft_in"), sem("exp_ready")
        xT_lo_ready, routed_ready, r_turned, r_copied = sem("xT_lo_ready"), sem("routed_ready"), sem("r_turned"), sem("r_copied")
        w_hi_ready, w_lo_ready = sem("w_hi_ready"), sem("w_lo_ready")
        h_made, h_ready, h_lo_ready, h_used = sem("h_made"), sem("h_ready"), sem("h_lo_ready"), sem("h_used")
        r_spread, r_b_ready, y_scaled, y_added = sem("r_spread"), sem("r_b_ready"), sem("y_scaled"), sem("y_added")
        y_turned, result_ready = sem("y_turned"), sem("result_ready")
        dve_step = sem("dve_step")

        def width(b):
            return BLOCK_TILES[b] * P

        def tiles(b):
            return slice(FIRST_TILE[b], FIRST_TILE[b] + BLOCK_TILES[b])

        def span(b):
            return slice(FIRST_TILE[b] * P, (FIRST_TILE[b] + BLOCK_TILES[b]) * P)

        def max_pair(b, s):
            return SPAIR[1] if b == 0 and s % 2 else MPAIR

        def slots_at(b, i):
            if b + 1 == NB:
                return []
            s = i - FIRST_SLOT_UNIT
            return [s] if 0 <= s < len(SLOTS[b + 1]) else []

        assert all(len(SLOTS[b + 1]) + FIRST_SLOT_UNIT < MAX_ROW_UNIT for b in range(NB - 1))
        assert POST["copy_r"] < UNITS

        def bank_of_hidden(u):
            return ps[:, u % 4, :]

        def ex_pair(buf, slot, chunks, n):
            return buf[:, slot, 0:len(chunks) * n].rearrange("p (k n) -> p k n", n=n)

        def hid(buf, u, n):
            return buf[:, u % P_RING, 0:n]

        block = stack.enter_context(nc.Block())

        @block.sync
        def _(sync):
            sync.dma_start(tok[:, :, :], xv).then_inc(x_in, 16)
            for g in range(NG):
                js = group_chunks(g)
                whole = min(js[-1] + 1, FULL)
                sync.dma_start(raw[:, js[0]:whole, :], ctxv[:, js[0]:whole, :]).then_inc(ctx_in[g], 16)
            sync.wait_ge(pad_zeroed, 1)
            sync.dma_start(raw[0:TAIL, FULL, :], ctx[0, FULL * P:NKEY, :]).then_inc(ctx_in[NG - 1], 16)
            for e in range(E):
                if e >= W_RING:
                    sync.wait_ge(w_lo_ready, e - W_RING + 1)
                slot, landed = w_raw[:, e % W_RING, :, :], w_in[e % W_RING]
                sync.dma_start(slot[:, 0, :], w1[e]).then_inc(landed, 16)
                sync.dma_start(slot[:, 1, :].rearrange("p (c d) -> p c d", d=D),
                               w2[e].rearrange("(c p) d -> p c d", p=P)).then_inc(landed, 16)
            for k, b in enumerate(FFN_ORDER):
                sync.wait_ge(result_ready, k + 1)
                sync.dma_start(outv[:, tiles(b), :], result[:, tiles(b), :]).then_inc(out_done, 16)
            sync.wait_ge(out_done, 16 * NB)

        @block.gpsimd
        def _(pool):
            steps = [0]

            def step(ins):
                steps[0] += 1
                ins.then_inc(pool_step, 1)
                pool.wait_ge(pool_step, steps[0])

            step(nc.gpsimd.memset(ident[:, :], 0.0))
            nc.gpsimd.affine_select(out=ident[:, :], in_=ident[:, :], compare_op=ALU.not_equal, fill=1.0,
                                    base=0, pattern=[[-1, P]], channel_multiplier=1).then_inc(ident_ready, 1)
            nc.gpsimd.memset(raw[:, FULL, :], 0.0).then_inc(pad_zeroed, 1)
            nc.gpsimd.memset(minus_half[:, :], -0.5)
            step(nc.gpsimd.memset(wv_sb[:, HID:HID + 1], 0.0))
            step(nc.gpsimd.memset(wv_sb[C:CA, HID:HID + 1], 1.0))
            step(nc.gpsimd.memset(ctxT_hi[C:CA, 0:NKEY].bitcast(F32), 1.0))
            step(nc.gpsimd.memset(ctxT_hi[C:CA, NKEY:NC * P].bitcast(F32), 0.0))
            nc.gpsimd.memset(ch[:, 0:FULL, C].bitcast(F32), 1.0)
            step(nc.gpsimd.memset(ch[:, FULL, C:CA].bitcast(F32), 0.0))
            nc.gpsimd.memset(ch[0:TAIL, FULL, C:CA].bitcast(F32), 1.0).then_inc(ones_ready, 1)
            pool.wait_ge(ones_ready, 1)
            nc.gpsimd.memset(earlier[:, :, :], 1.0)
            step(nc.gpsimd.memset(sel_f, 0.0))
            nc.gpsimd.affine_select(out=earlier[:, :, :], in_=earlier[:, :, :], compare_op=ALU.is_gt, fill=0.0,
                                    base=0, pattern=[[1, E], [-1, E]], channel_multiplier=0)
            for half in range(2):
                step(nc.gpsimd.affine_select(out=sel_f, in_=sel_f, compare_op=ALU.not_equal,
                                             fill=1.0, base=-E * half, pattern=[[-1, E], [0, P]],
                                             channel_multiplier=1))
            nc.gpsimd.tensor_copy(sel[:, :, :], sel_f).then_inc(sel_ready, 1)

            def inverse_deviation(k):
                which, b = k // NB, k % NB
                pool.wait_ge(var_ready, k + 1)
                nc.gpsimd.tensor_tensor(rstd[:, which, tiles(b)], veps[:, which, tiles(b)],
                                        minus_half[:, tiles(b)], ALU.pow).then_inc(rstd_ready, 1)

            inverse_deviation(0)
            for g in range(NG):
                js = group_chunks(g)
                pool.wait_ge(ctx_hi_ready, g + 1)
                nc.gpsimd.tensor_tensor(cl[:, js[0]:js[-1] + 1, :], raw[:, js[0]:js[-1] + 1, :],
                                        ch[:, js[0]:js[-1] + 1, 0:C].bitcast(F32),
                                        ALU.subtract).then_inc(ctx_lo_ready, 1)
                if g + 1 < NB:
                    inverse_deviation(g + 1)
            for b in range(NB - 1):
                inverse_deviation(NB + b)

            def add_output(k, e):
                b = FFN_ORDER[k]
                if e:
                    pool.wait_ge(y_scaled, k * E + e + 1)
                    if e > 1:
                        pool.wait_ge(y_added, k * (E - 1) + e - 1)
                    nc.gpsimd.tensor_tensor(acc[:, span(b)], acc[:, span(b)], y_r[:, e % 2, 0:width(b)],
                                            ALU.add).then_inc(y_added, 1)

            for e in range(E):
                pool.wait_ge(w_hi_ready, e + 1)
                nc.gpsimd.tensor_tensor(w1_lo[:, e * H:(e + 1) * H], w_raw[:, e % W_RING, 0, :],
                                        w1_hi[:, e * H:(e + 1) * H].bitcast(F32), ALU.subtract)
                nc.gpsimd.tensor_tensor(w2_lo[:, e, :, :].rearrange("p c d -> p (c d)"),
                                        w_raw[:, e % W_RING, 1, :],
                                        w2_hi[:, e, :, :].rearrange("p c d -> p (c d)").bitcast(F32),
                                        ALU.subtract).then_inc(w_lo_ready, 1)
                if e == 1:
                    inverse_deviation(2 * NB - 1)
                if e >= 2:
                    add_output(0, e - 2)
            for e in range(E - 2, E):
                add_output(0, e)
            for k in range(1, NB):
                for e in range(E):
                    add_output(k, e)

        @block.scalar
        def _(act):
            act.dma_start(rows[0:E * HC, :], b1.rearrange("e (c p) -> (e c) p", p=P)).then_inc(small_in, 16)
            act.dma_start(rows[E * HC:E * HC + E, :], b2).then_inc(small_in, 16)
            act.dma_start(rows[E * HC + E:NROW, :], bq.rearrange("(a h) -> a h", a=1)).then_inc(small_in, 16)
            act.dma_start(wk_sb[0:C, :], wk).then_inc(small_in, 16)
            act.dma_start(wk_sb[C:CA, :], bk.rearrange("(a h) -> a h", a=1)).then_inc(small_in, 16)
            act.dma_start(wq_sb[:, :], wq).then_inc(w_consts_in, 16)
            act.dma_start(wv_sb[0:C, 0:HID], wv).then_inc(w_consts_in, 16)
            act.dma_start(wv_sb[C:CA, 0:HID], bv.rearrange("(a h) -> a h", a=1)).then_inc(w_consts_in, 16)
            act.dma_start(wr_sb[:, :], wr).then_inc(w_consts_in, 16)
            act.dma_start(br_sb[:, :], br.rearrange("(a e) -> a e", a=1).partition_broadcast(P)).then_inc(w_consts_in, 16)
            act.dma_start(gates[:, 0:1], g_xattn.rearrange("(a e) -> a e", a=1).partition_broadcast(P)).then_inc(w_consts_in, 16)
            act.dma_start(gates[:, 1:2], g_ffn.rearrange("(a e) -> a e", a=1).partition_broadcast(P)).then_inc(w_consts_in, 16)
            act.wait_ge(small_turned, 1)
            nc.scalar.copy(cols[:, :], UB[1][:, 0:NROW])
            nc.scalar.copy(wkT[:, :], UB[1][:, 64:64 + CA]).then_inc(small_copied, 1)

            def copy_ctx(g):
                js = group_chunks(g)
                w = len(js) * P
                act.wait_ge(ctx_turned, g + 1)
                nc.scalar.copy(ctxT_hi[0:C, js[0] * P:js[0] * P + w],
                               SPAIR[0].rearrange("p k n -> p (k n)")[0:C, 0:w]).then_inc(ctxT_hi_ready, 1)
                nc.scalar.copy(ch[:, js[0]:js[-1] + 1, 0:C], raw[:, js[0]:js[-1] + 1, :]).then_inc(ctx_hi_ready, 1)

            def copy_x(b):
                act.wait_ge(x_turned, b + 1)
                nc.scalar.copy(xT[:, span(b)], UB[0][:, 0:width(b)]).then_inc(x_copied, 1)

            def copy_q(b):
                act.wait_ge(q_made, b + 1)
                nc.scalar.activation(qT[:, 0:width(b)], UB[1][:, 0:width(b)], ACT.Identity,
                                     bias=cols[:, NROW - 1:NROW]).then_inc(q_copied, 1)

            def copy_qk(b):
                act.wait_ge(qk_made, b + 1)
                nc.scalar.activation(q_f[:, span(b)], UB[0][0:CA, 0:width(b)], ACT.Copy, scale=SCALE)
                nc.scalar.activation(q_hi[:, span(b)], UB[0][0:CA, 0:width(b)], ACT.Copy,
                                     scale=SCALE).then_inc(qk_copied, 1)

            copy_ctx(0)
            copy_x(0)
            copy_q(0)
            copy_ctx(1)
            copy_qk(0)
            act.wait_ge(w_consts_in, 7 * 16)
            nc.scalar.activation(tanh_g[:, :], gates[:, :], ACT.Tanh).then_inc(tanh_ready, 1)
            for g in range(2, NG):
                copy_ctx(g)
                b = g - 3
                if 1 <= b < NB:
                    copy_x(b)
                    copy_q(b)
                    copy_qk(b)

            def post(b, i):
                n = width(b)
                if i == POST["u_copy"]:
                    act.wait_ge(ex_used, (b + 1) * UNITS)
                    nc.scalar.copy(u_sb[:, 0:n], UB[b % 2][0:CA, 0:n]).then_inc(u_copied, 1)
                if i == POST["turn"]:
                    act.wait_ge(x_turned, NB + b + 1)
                    nc.scalar.copy(xT[:, span(b)], UB[b % 2][:, 0:n])
                    nc.scalar.copy(xT_hi[:, span(b)], UB[b % 2][:, 0:n]).then_inc(x_copied, 1)
                if i == POST["soft2"]:
                    act.wait_ge(soft_in, b + 1)
                    nc.scalar.activation(le[:, tiles(b), :], ld[:, tiles(b), :], ACT.Exp).then_inc(exp_ready, 1)
                if i == POST["copy_r"]:
                    act.wait_ge(r_turned, b + 1)
                    nc.scalar.copy(rT[:, span(b)], UB[b % 2][0:2 * E, 0:n]).then_inc(r_copied, 1)

            for b in range(NB):
                n = width(b)
                for i in range(UNITS):
                    u = b * UNITS + i
                    js = unit_chunks(i)
                    act.wait_ge(scores_ready, u + 1)
                    if u >= P_RING:
                        act.wait_ge(ex_used, u - P_RING + 1)
                        act.wait_ge(lo_ready, u - P_RING + 1)
                    scores = SPAIR[u % 2][:, 0:len(js), 0:n]
                    nc.scalar.activation(ex_pair(ex, u % P_RING, js, n), scores, ACT.Exp)
                    nc.scalar.activation(ex_pair(ex_hi, u % P_RING, js, n), scores, ACT.Exp).then_inc(ex_ready, 1)
                    if b:
                        post(b - 1, i)

            for k, b in enumerate(FFN_ORDER):
                n = width(b)
                for i in range(FU):
                    u = k * FU + i
                    if i % HC == 0:
                        act.wait_ge(r_spread, k * E + i // HC + 1)
                        if k * E + i // HC >= 2:
                            act.wait_ge(y_scaled, k * E + i // HC - 1)
                        nc.scalar.copy(r_b[:, (i // HC) % 2, 0:n], UB[1][:, 0:n]).then_inc(r_b_ready, 1)
                    act.wait_ge(h_made, u + 1)
                    if u >= P_RING:
                        act.wait_ge(h_used, u - P_RING + 1)
                        act.wait_ge(h_lo_ready, u - P_RING + 1)
                    else:
                        act.wait_ge(ex_used, NB * UNITS)
                    src = bank_of_hidden(u)[:, 0:n]
                    nc.scalar.activation(hid(ex, u, n), src, ACT.Relu, bias=cols[:, i:i + 1])
                    nc.scalar.activation(hid(ex_hi, u, n), src, ACT.Relu, bias=cols[:, i:i + 1]).then_inc(h_ready, 1)
                    if k == 0:
                        post(NB - 1, i)

        @block.vector
        def _(dve):
            steps = [0]

            def step(ins):
                steps[0] += 1
                ins.then_inc(dve_step, 1)
                dve.wait_ge(dve_step, steps[0])

            def statistics(which, b):
                for t in range(BLOCK_TILES[b]):
                    last = nc.vector.bn_stats(stats[:, which, FIRST_TILE[b] + t, :], tok[:, FIRST_TILE[b] + t, :])
                step(last)
                for t in range(BLOCK_TILES[b]):
                    last = nc.vector.bn_aggr(mv[:, which, FIRST_TILE[b] + t, :], stats[:, which, FIRST_TILE[b] + t, :])
                step(last)
                nc.vector.tensor_scalar(veps[:, which, tiles(b)], mv[:, which, tiles(b), 1], EPS, None,
                                        ALU.add).then_inc(var_ready, 1)

            def normalize(which, b):
                dve.wait_ge(rstd_ready, which * NB + b + 1)
                for t in range(FIRST_TILE[b], FIRST_TILE[b] + BLOCK_TILES[b]):
                    last = nc.vector.tensor_scalar(norm[:, t, :], tok[:, t, :], mv[:, which, t, 0:1],
                                                   rstd[:, which, t:t + 1], ALU.subtract, ALU.mult)
                last.then_inc(norm_ready, 1)

            def split_ctxT(g):
                js = group_chunks(g)
                w = len(js) * P
                dve.wait_ge(ctxT_hi_ready, g + 1)
                nc.vector.tensor_tensor(ctxT_lo[0:C, js[0] * P:js[0] * P + w],
                                        SPAIR[0].rearrange("p k n -> p (k n)")[0:C, 0:w],
                                        ctxT_hi[0:C, js[0] * P:js[0] * P + w].bitcast(F32),
                                        ALU.subtract).then_inc(ctxT_lo_ready, 1)

            def split_q(b):
                dve.wait_ge(qk_copied, b + 1)
                nc.vector.tensor_tensor(q_lo[:, span(b)], q_f[0:C, span(b)], q_hi[0:C, span(b)].bitcast(F32),
                                        ALU.subtract).then_inc(q_lo_ready, 1)

            def reduce_max(b, s):
                ts, _, w, place = SLOTS[b][s]
                dve.wait_ge(max_scores, SLOTS_BEFORE[b] + s + 1)
                t0 = FIRST_TILE[b] + ts[0]
                pair = max_pair(b, s)
                if place < NMAX - 1:
                    ins = nc.vector.tensor_reduce(pmax[:, t0, place:place + 1], pair[:, :, 0:w], AX.XY, ALU.max)
                else:
                    ins = nc.vector.tensor_reduce(pmax[:, t0:t0 + len(ts), place], pair[:, 0:len(ts), 0:w],
                                                  AX.X, ALU.max)
                ins.then_inc(max_reduced, 1)

            def finish_max(b):
                dve.wait_ge(max_reduced, SLOTS_BEFORE[b] + len(SLOTS[b]))
                nc.vector.tensor_reduce(nmax[:, tiles(b)], pmax[:, tiles(b), :], AX.X, ALU.max,
                                        negate=True).then_inc(nmax_ready, 1)

            def row_max(b):
                dve.wait_ge(max_row, b + 1)
                nc.vector.tensor_tensor(q_hi[C:CA, span(b)], MPAIR[C:CA, 0, 0:width(b)], q_f[C:CA, span(b)],
                                        ALU.add).then_inc(row_ready, 1)

            dve.wait_ge(x_in, 16)
            statistics(0, 0)
            split_ctxT(0)
            normalize(0, 0)
            split_ctxT(1)
            split_q(0)
            first = SLOTS[0]
            nb0 = BLOCK_TILES[0]
            for g in range(1, NG):
                if g > 1:
                    split_ctxT(g)
                if g < NB:
                    statistics(0, g)
                for s in range((g - 1) * nb0, g * nb0):
                    reduce_max(0, s)
                if g < NB:
                    normalize(0, g)
                b = g - 3
                if 1 <= b < NB:
                    split_q(b)
            for s in range((NG - 1) * nb0, len(first)):
                reduce_max(0, s)
            finish_max(0)
            for b in range(max(1, NG - 3), NB):
                split_q(b)
            row_max(0)

            def post(b, i):
                n, ts = width(b), tiles(b)
                nt = BLOCK_TILES[b]
                bank = UB[b % 2]
                if i == POST["residual"]:
                    dve.wait_ge(projected, b + 1)
                    proj = bank[:, 0:nt * (HID + 1)].rearrange("p (t h) -> p t h", h=HID + 1)
                    step(nc.vector.reciprocal(rsum[:, ts], proj[:, :, HID]))
                    dve.wait_ge(tanh_ready, 1)
                    step(nc.vector.tensor_scalar(gsum[:, ts], rsum[:, ts], tanh_g[:, 0:1], None, ALU.mult))
                    for t in range(nt):
                        ft = FIRST_TILE[b] + t
                        last = nc.vector.scalar_tensor_tensor(out=tok[:, ft, :], in0=proj[:, t, 0:HID],
                                                              scalar=gsum[:, ft:ft + 1], in1=tok[:, ft, :],
                                                              op0=ALU.mult, op1=ALU.add)
                    step(last)
                    statistics(1, b)
                if i == POST["normalize"]:
                    normalize(1, b)
                if i == POST["split"]:
                    dve.wait_ge(x_copied, NB + b + 1)
                    nc.vector.tensor_tensor(xT_lo[:, span(b)], xT[:, span(b)], xT_hi[:, span(b)].bitcast(F32),
                                            ALU.subtract).then_inc(xT_lo_ready, 1)
                if i == POST["soft1"]:
                    dve.wait_ge(logits_ready, b + 1)
                    dve.wait_ge(w_consts_in, 7 * 16)
                    step(nc.vector.tensor_tensor(lg[:, ts, :], bank[:, 0:nt * E].rearrange("p (t e) -> p t e", e=E),
                                                 br_sb[:, :].unsqueeze(1).to_broadcast([P, nt, E]), ALU.add))
                    step(nc.vector.tensor_reduce(lmax[:, ts], lg[:, ts, :], AX.X, ALU.max))
                    nc.vector.tensor_tensor(ld[:, ts, :], lg[:, ts, :],
                                            lmax[:, ts].unsqueeze(2).to_broadcast([P, nt, E]),
                                            ALU.subtract).then_inc(soft_in, 1)
                    own = lg[:, ts, :].unsqueeze(3).to_broadcast([P, nt, E, E])
                    other = lg[:, ts, :].unsqueeze(2).to_broadcast([P, nt, E, E])
                    nc.vector.tensor_tensor(cmp_gt[:, 0:nt, :, :], other, own, ALU.is_gt)
                    step(nc.vector.tensor_tensor(cmp_eq[:, 0:nt, :, :], other, own, ALU.is_equal))
                    step(nc.vector.tensor_tensor(cmp_eq[:, 0:nt, :, :], cmp_eq[:, 0:nt, :, :],
                                                 earlier[:, :, :].unsqueeze(1).to_broadcast([P, nt, E, E]),
                                                 ALU.mult))
                    step(nc.vector.tensor_tensor(cmp_gt[:, 0:nt, :, :], cmp_gt[:, 0:nt, :, :],
                                                 cmp_eq[:, 0:nt, :, :], ALU.add))
                    nc.vector.tensor_reduce(rank[:, ts, :], cmp_gt[:, 0:nt, :, :], AX.X, ALU.add)
                if i == POST["soft3"]:
                    dve.wait_ge(exp_ready, b + 1)
                    step(nc.vector.tensor_reduce(esum[:, ts], le[:, ts, :], AX.X, ALU.add))
                    step(nc.vector.reciprocal(einv[:, ts], esum[:, ts]))
                    step(nc.vector.tensor_tensor(le[:, ts, :], le[:, ts, :],
                                                 einv[:, ts].unsqueeze(2).to_broadcast([P, nt, E]), ALU.mult))
                    step(nc.vector.scalar_tensor_tensor(out=picked[:, ts, :], in0=rank[:, ts, :], scalar=2.0,
                                                        in1=le[:, ts, :], op0=ALU.is_lt, op1=ALU.mult))
                    step(nc.vector.tensor_reduce(psumw[:, ts], picked[:, ts, :], AX.X, ALU.add))
                    step(nc.vector.reciprocal(pinv[:, ts], psumw[:, ts]))
                    step(nc.vector.tensor_tensor(routed[:, ts, :], picked[:, ts, :],
                                                 pinv[:, ts].unsqueeze(2).to_broadcast([P, nt, E]), ALU.mult))
                    step(nc.vector.tensor_copy(r_hi[:, ts, :], routed[:, ts, :]))
                    nc.vector.tensor_copy(r_cat[:, ts, 0:E], r_hi[:, ts, :].bitcast(F32))
                    nc.vector.tensor_tensor(r_cat[:, ts, E:2 * E], routed[:, ts, :], r_hi[:, ts, :].bitcast(F32),
                                            ALU.subtract).then_inc(routed_ready, 1)

            for b in range(NB):
                n = width(b)
                for i in range(UNITS):
                    u = b * UNITS + i
                    js = unit_chunks(i)
                    dve.wait_ge(ex_ready, u + 1)
                    if u >= P_RING:
                        dve.wait_ge(ex_used, u - P_RING + 1)
                    m = len(js) * n
                    nc.vector.tensor_tensor(ex_lo[:, u % P_RING, 0:m], ex[:, u % P_RING, 0:m],
                                            ex_hi[:, u % P_RING, 0:m].bitcast(F32), ALU.subtract).then_inc(lo_ready, 1)
                    for s in slots_at(b, i):
                        reduce_max(b + 1, s)
                    if b + 1 < NB and i == MAX_ROW_UNIT - 1:
                        finish_max(b + 1)
                    if b + 1 < NB and i == MAX_ROW_UNIT:
                        row_max(b + 1)
                    if b:
                        post(b - 1, i)

            def round_weights(e):
                if e == 0:
                    dve.wait_ge(ex_used, NB * UNITS)
                dve.wait_ge(w_in[e % W_RING], 32 * (e // W_RING + 1))
                nc.vector.tensor_copy(w1_hi[:, e * H:(e + 1) * H], w_raw[:, e % W_RING, 0, :])
                nc.vector.tensor_copy(w2_hi[:, e, :, :].rearrange("p c d -> p (c d)"),
                                      w_raw[:, e % W_RING, 1, :]).then_inc(w_hi_ready, 1)

            def scale_output(k, e):
                b = FFN_ORDER[k]
                n = width(b)
                dve.wait_ge(h_used, k * FU + (e + 1) * HC)
                dve.wait_ge(r_b_ready, k * E + e + 1)
                if e > 2 or (k and e > 0):
                    before = k * (E - 1) + max(e - 2, 0)
                    if before > 0:
                        dve.wait_ge(y_added, before)
                dst = y_r[:, e % 2, 0:n] if e else acc[:, span(b)]
                nc.vector.scalar_tensor_tensor(out=dst, in0=MPAIR[:, e % 2, 0:n],
                                               scalar=cols[:, E * HC + e:E * HC + e + 1],
                                               in1=r_b[:, e % 2, 0:n], op0=ALU.add, op1=ALU.mult).then_inc(y_scaled, 1)

            def finish_block(k):
                b = FFN_ORDER[k]
                dve.wait_ge(y_turned, k + 1)
                nt = BLOCK_TILES[b]
                src = UB[0][:, 0:nt * P].rearrange("p (t d) -> p t d", d=P)
                nc.vector.scalar_tensor_tensor(out=result[:, tiles(b), :], in0=src, scalar=tanh_g[:, 1:2],
                                               in1=tok[:, tiles(b), :], op0=ALU.mult, op1=ALU.add).then_inc(result_ready, 1)

            round_weights(0)
            round_weights(1)
            for k, b in enumerate(FFN_ORDER):
                n = width(b)
                for i in range(FU):
                    u = k * FU + i
                    e = i // HC
                    if k == 0 and i % HC == 0 and 2 <= e + 1 < E:
                        round_weights(e + 1)
                    dve.wait_ge(h_ready, u + 1)
                    if u >= P_RING:
                        dve.wait_ge(h_used, u - P_RING + 1)
                    nc.vector.tensor_tensor(hid(ex_lo, u, n), hid(ex, u, n), hid(ex_hi, u, n).bitcast(F32),
                                            ALU.subtract).then_inc(h_lo_ready, 1)
                    if i % HC == LAG and e > 0:
                        scale_output(k, e - 1)
                    if i == LAG and k > 0:
                        scale_output(k - 1, E - 1)
                    if i == 2 * HC and k > 0:
                        finish_block(k - 1)
                    if k == 0:
                        post(NB - 1, i)
            scale_output(NB - 1, E - 1)
            finish_block(NB - 1)

        @block.tensor
        def _(pe):
            pe.wait_ge(ident_ready, 1)
            pe.wait_ge(small_in, 5 * 16)
            nc.tensor.transpose(UB[1][:, 0:NROW], rows[:, :], ident[0:NROW, 0:NROW])
            nc.tensor.transpose(UB[1][:, 64:64 + CA], wk_sb[:, :], ident[0:CA, 0:CA]).then_inc(small_turned, 1)

            def turn_ctx(g):
                js = group_chunks(g)
                pe.wait_ge(ctx_in[g], 16 if js[-1] < FULL else 32)
                if g:
                    pe.wait_ge(ctxT_lo_ready, g)
                flat = SPAIR[0].rearrange("p k n -> p (k n)")
                for k, j in enumerate(js):
                    last = nc.tensor.transpose(flat[0:C, k * P:(k + 1) * P], raw[:, j, :], ident[:, :])
                last.then_inc(ctx_turned, 1)

            def turn_x(which, b, bank):
                pe.wait_ge(norm_ready, which * NB + b + 1)
                for t in range(BLOCK_TILES[b]):
                    last = nc.tensor.transpose(bank[:, t * P:(t + 1) * P], norm[:, FIRST_TILE[b] + t, :], ident[:, :])
                last.then_inc(x_turned, 1)

            def make_q(b):
                pe.wait_ge(small_copied, 1)
                pe.wait_ge(w_consts_in, 7 * 16)
                pe.wait_ge(x_copied, b + 1)
                nc.tensor.matmul(UB[1][:, 0:width(b)], wq_sb[:, :], xT[:, span(b)], start=True, stop=True).then_inc(q_made, 1)

            def make_qk(b):
                pe.wait_ge(q_copied, b + 1)
                nc.tensor.matmul(UB[0][0:CA, 0:width(b)], wkT[:, :], qT[:, 0:width(b)], start=True,
                                 stop=True).then_inc(qk_made, 1)

            def score_for_max(b, s):
                ts, key0, w, place = SLOTS[b][s]
                pair = max_pair(b, s)
                if b == 0:
                    if s >= 2:
                        pe.wait_ge(max_reduced, s - 1)
                else:
                    pe.wait_ge(row_ready, b)
                    pe.wait_ge(max_reduced, SLOTS_BEFORE[b] + s)
                for k in range(2 if place < NMAX - 1 else len(ts)):
                    t = FIRST_TILE[b] + (ts[0] if place < NMAX - 1 else ts[k])
                    key = key0 + (k * BANK if place < NMAX - 1 else 0)
                    last = nc.tensor.matmul(pair[:, k, 0:w], q_hi[:, t * P:(t + 1) * P], ctxT_hi[0:CA, key:key + w],
                                            start=True, stop=True)
                last.then_inc(max_scores, 1)

            def turn_max(b):
                pe.wait_ge(nmax_ready, b + 1)
                for t in range(BLOCK_TILES[b]):
                    ft = FIRST_TILE[b] + t
                    last = nc.tensor.matmul(MPAIR[C:CA, 0, t * P:(t + 1) * P], nmax[:, ft:ft + 1], ident[:, :],
                                            start=True, stop=True)
                last.then_inc(max_row, 1)

            def q_chain(b):
                if b > 0:
                    pe.wait_ge(qk_copied, b)
                turn_x(0, b, UB[0])
                make_q(b)
                make_qk(b)

            nb0 = BLOCK_TILES[0]
            turn_ctx(0)
            turn_x(0, 0, UB[0])
            make_q(0)
            turn_ctx(1)
            make_qk(0)
            pe.wait_ge(qk_copied, 1)
            for g in range(1, NG):
                if g > 1:
                    turn_ctx(g)
                if g == 1:
                    pe.wait_ge(ones_ready, 1)
                for s in range((g - 1) * nb0, g * nb0):
                    score_for_max(0, s)
                b = g - 3
                if 1 <= b < NB:
                    q_chain(b)
            pe.wait_ge(ctxT_hi_ready, NG)
            for s in range((NG - 1) * nb0, len(SLOTS[0])):
                score_for_max(0, s)
            turn_max(0)

            def scores(b, i):
                u = b * UNITS + i
                n = width(b)
                if i == 0:
                    pe.wait_ge(row_ready, b + 1)
                    pe.wait_ge(q_lo_ready, b + 1)
                if u == 0:
                    pe.wait_ge(ctxT_lo_ready, NG)
                if u >= 2:
                    pe.wait_ge(ex_ready, u - 1)
                for k, j in enumerate(unit_chunks(i)):
                    dst = SPAIR[u % 2][:, k, 0:n]
                    keys = slice(j * P, (j + 1) * P)
                    nc.tensor.matmul(dst, ctxT_hi[0:CA, keys], q_hi[:, span(b)], start=True, stop=False)
                    nc.tensor.matmul(dst, ctxT_hi[0:C, keys], q_lo[:, span(b)], start=False, stop=False)
                    last = nc.tensor.matmul(dst, ctxT_lo[0:C, keys], q_hi[0:C, span(b)], start=False, stop=True)
                last.then_inc(scores_ready, 1)

            def values(b, i):
                u = b * UNITS + i
                n = width(b)
                js = unit_chunks(i)
                dst = UB[b % 2]
                pe.wait_ge(lo_ready, u + 1)
                if b == 0:
                    g = js[-1] // TRANSPOSE_GROUP
                    pe.wait_ge(ctx_lo_ready, g + 1)
                if i == 0 and b >= 2:
                    pe.wait_ge(r_copied, b - 1)
                for k, j in enumerate(js):
                    hi = ex_hi[:, u % P_RING, k * n:(k + 1) * n]
                    lo = ex_lo[:, u % P_RING, k * n:(k + 1) * n]
                    nc.tensor.matmul(dst[0:CA, 0:n], ch[:, j, :], hi, start=(j == 0), stop=False)
                    nc.tensor.matmul(dst[0:C, 0:n], cl[:, j, :], hi, start=False, stop=False)
                    last = nc.tensor.matmul(dst[0:CA, 0:n], ch[:, j, :], lo, start=False, stop=(j == NC - 1))
                last.then_inc(ex_used, 1)

            def post(b, i):
                n, nt = width(b), BLOCK_TILES[b]
                bank = UB[b % 2]
                if i == POST["project"]:
                    pe.wait_ge(u_copied, b + 1)
                    for t in range(nt):
                        last = nc.tensor.matmul(bank[:, t * (HID + 1):(t + 1) * (HID + 1)], u_sb[:, t * P:(t + 1) * P],
                                                wv_sb[:, :], start=True, stop=True)
                    last.then_inc(projected, 1)
                if i == POST["turn"]:
                    turn_x(1, b, bank)
                if i == POST["logits"]:
                    pe.wait_ge(x_copied, NB + b + 1)
                    for t in range(nt):
                        ft = FIRST_TILE[b] + t
                        last = nc.tensor.matmul(bank[:, t * E:(t + 1) * E], xT[:, ft * P:(ft + 1) * P], wr_sb[:, :],
                                                start=True, stop=True)
                    last.then_inc(logits_ready, 1)
                if i == POST["turn_r"]:
                    pe.wait_ge(routed_ready, b + 1)
                    for t in range(nt):
                        last = nc.tensor.transpose(bank[0:2 * E, t * P:(t + 1) * P], r_cat[:, FIRST_TILE[b] + t, :],
                                                   ident[:, :])
                    last.then_inc(r_turned, 1)

            for v in range(NB * UNITS + LAG):
                b, i = divmod(v, UNITS)
                if b < NB:
                    scores(b, i)
                    for s in slots_at(b, i):
                        score_for_max(b + 1, s)
                    if b + 1 < NB and i == MAX_ROW_UNIT:
                        turn_max(b + 1)
                    if b:
                        post(b - 1, i)
                if v >= LAG:
                    values(*divmod(v - LAG, UNITS))

            def hidden(k, i):
                b, u = FFN_ORDER[k], k * FU + i
                n = width(b)
                e = i // HC
                if i % HC == 0:
                    if k == 0:
                        pe.wait_ge(w_lo_ready, e + 1)
                    if i == 0:
                        pe.wait_ge(xT_lo_ready, b + 1)
                        pe.wait_ge(r_copied, b + 1)
                        pe.wait_ge(sel_ready, 1)
                    if k * E + e >= 1:
                        pe.wait_ge(r_b_ready, k * E + e)
                    nc.tensor.matmul(UB[1][:, 0:n], sel[:, e, :], rT[:, span(b)], start=True, stop=True).then_inc(r_spread, 1)
                if u >= 4:
                    pe.wait_ge(h_ready, u - 3)
                dst = bank_of_hidden(u)[:, 0:n]
                rows_ = slice(i * P, (i + 1) * P)
                nc.tensor.matmul(dst, w1_hi[:, rows_], xT_hi[:, span(b)], start=True, stop=False)
                nc.tensor.matmul(dst, w1_hi[:, rows_], xT_lo[:, span(b)], start=False, stop=False)
                nc.tensor.matmul(dst, w1_lo[:, rows_], xT_hi[:, span(b)], start=False, stop=True).then_inc(h_made, 1)

            def expert_out(k, i):
                b, u = FFN_ORDER[k], k * FU + i
                n = width(b)
                e, c = divmod(i, HC)
                pe.wait_ge(h_lo_ready, u + 1)
                if c == 0 and k * E + e >= 2:
                    pe.wait_ge(y_scaled, k * E + e - 1)
                dst = MPAIR[:, e % 2, 0:n]
                hi, lo = hid(ex_hi, u, n), hid(ex_lo, u, n)
                nc.tensor.matmul(dst, w2_hi[:, e, c, :], hi, start=(c == 0), stop=False)
                nc.tensor.matmul(dst, w2_hi[:, e, c, :], lo, start=False, stop=False)
                nc.tensor.matmul(dst, w2_lo[:, e, c, :], hi, start=False, stop=(c == HC - 1)).then_inc(h_used, 1)

            def turn_output(k):
                b = FFN_ORDER[k]
                pe.wait_ge(y_added, (k + 1) * (E - 1))
                pe.wait_ge(r_copied, NB)
                if k:
                    pe.wait_ge(result_ready, k)
                for t in range(BLOCK_TILES[b]):
                    ft = FIRST_TILE[b] + t
                    last = nc.tensor.transpose(UB[0][:, t * P:(t + 1) * P], acc[:, ft * P:(ft + 1) * P], ident[:, :])
                last.then_inc(y_turned, 1)

            for v in range(NB * FU + LAG):
                k, i = divmod(v, FU)
                if k < NB:
                    hidden(k, i)
                    if k == 0:
                        post(NB - 1, i)
                    if k > 0 and i == 2 * HC - 1:
                        turn_output(k - 1)
                if v >= LAG:
                    expert_out(*divmod(v - LAG, FU))
            turn_output(NB - 1)


_INS = ['x', 'ctx_768', 'g_xattn', 'g_ffn', 'L0_xattn_Wq', 'L0_xattn_bq', 'L0_xattn_Wk', 'L0_xattn_bk',
        'L0_xattn_Wv', 'L0_xattn_bv', 'L0_ffn_W1', 'L0_ffn_b1', 'L0_ffn_W2', 'L0_ffn_b2', 'L0_ffn_Wr',
        'L0_ffn_br']
_OUTS = [((1, 1024, 128), 'float32')]


def kernel(**inputs):
    import numpy as _np
    import concourse.bacc as _bacc
    from concourse import mybir as _mybir
    from concourse.bass_utils import run_bass_kernel_spmd as _run

    nc = _bacc.Bacc("TRN2", target_bir_lowering=False, num_devices=1)
    arrays, args = {}, []
    for name in _INS:
        a = _np.ascontiguousarray(inputs[name])
        arrays[f"in_{name}_dram"] = a
        args.append(nc.dram_tensor(f"in_{name}_dram", a.shape, _mybir.dt.from_np(a.dtype), kind="ExternalInput").ap())
    for i, (shape, dtype) in enumerate(_OUTS):
        dt = _mybir.dt.from_np(_np.dtype(dtype))
        args.append(nc.dram_tensor(f"out_{i}_dram", shape, dt, kind="ExternalOutput").ap())
    attention_experts(nc, *args)
    r = _run(nc, [arrays], core_ids=[0])
    got = tuple(r.results[0][f"out_{i}_dram"] for i in range(len(_OUTS)))
    return got[0]
```

```python
from contextlib import ExitStack

import concourse.bass as bass
from concourse import mybir

F32 = mybir.dt.float32
F32R = mybir.dt.float32r
ALU = mybir.AluOpType
ACT = mybir.ActivationFunctionType
AX = mybir.AxisListType

P = 128
BANK = 512
BLOCK_TILES = [2, 3, 3]
NB = len(BLOCK_TILES)
FIRST_TILE = [sum(BLOCK_TILES[:b]) for b in range(NB)]
FFN_ORDER = [1, 0, 2]
TRANSPOSE_GROUP = 8
LAG = 2
P_RING = 3
H_LAG = 3
H_RING = 2 * P_RING
W_RING = 2
EPS = 1e-5

STEPS = ["u_copy", "project", "gate", "residual", "stats", "normalize", "turn", "split", "logits", "shift",
         "compare", "exp", "rank", "weights", "pick", "share", "turn_r", "copy_r"]
POST_ATTENTION = dict(zip(STEPS, [3, 5, 5, 6, 7, 9, 12, 13, 14, 15, 16, 17, 17, 18, 19, 20, 23, 24]))
POST_EXPERTS = dict(zip(STEPS, [2, 5, 7, 9, 11, 14, 19, 21, 22, 25, 27, 29, 29, 32, 34, 37, 43, 44]))


def attention_experts(nc, x, ctx, g_xattn, g_ffn, wq, bq, wk, bk, wv, bv, w1, b1, w2, b2, wr, br, out):
    _, NTOK, D = x.shape
    _, NKEY, C = ctx.shape
    HID = wq.shape[1]
    E, _, H = w1.shape
    NT = NTOK // P
    FULL = NKEY // P
    TAIL = NKEY - FULL * P
    NC = FULL + 1
    CA = C + 1
    NG = -(-NC // TRANSPOSE_GROUP)
    UNITS = -(-NC // 2)
    HC = H // P
    FU = E * HC
    SCALE = float(HID) ** -0.5
    MAXN = max(BLOCK_TILES) * P
    assert D == P and HID == P and sum(BLOCK_TILES) == NT and TAIL > 0 and C == 96

    xv = x.rearrange("a (p t) d -> p (a t) d", t=NT)
    outv = out.rearrange("a (p t) d -> p (a t) d", t=NT)
    ctxv = ctx[0, 0:FULL * P, :].rearrange("(p j) c -> p j c", j=FULL)

    def group_chunks(g):
        return range(g * TRANSPOSE_GROUP, min((g + 1) * TRANSPOSE_GROUP, NC))

    def unit_chunks(i):
        return range(2 * i, min(2 * i + 2, NC))

    NMAX = -(-NKEY // BANK)
    SLOTS = [[(t, w * BANK, min(BANK, NKEY - w * BANK), w) for w in range(NMAX) for t in range(n)]
             for n in BLOCK_TILES]
    SLOTS_BEFORE = [sum(len(s) for s in SLOTS[:b]) for b in range(NB)]
    MAX_ROW_UNIT = UNITS - 2

    def slots_at(b, i):
        if b + 1 == NB or i >= MAX_ROW_UNIT - 2:
            return []
        n = len(SLOTS[b + 1])
        return range(i * n // (MAX_ROW_UNIT - 2), (i + 1) * n // (MAX_ROW_UNIT - 2))

    def split_unit(e):
        last_chunk = ((e + 1) * H - 1) // C
        return last_chunk // 2

    with ExitStack() as stack:
        def sb(name, shape, dt=F32):
            return stack.enter_context(nc.sbuf_tensor(name, shape, dt))

        def sem(name):
            return stack.enter_context(nc.semaphore(name))

        raw = sb("raw", [P, NC, C])
        ctx_hi = sb("ctx_hi", [P, NC * CA], F32R)
        ctx_lo = sb("ctx_lo", [P, NC * C], F32R)
        ctxT_hi = sb("ctxT_hi", [P, NC * P], F32R)
        ctxT_lo = sb("ctxT_lo", [P, NC * P], F32R)
        ch = ctx_hi[:, :].rearrange("p (j c) -> p j c", c=CA)
        cl = ctx_lo[:, :].rearrange("p (j c) -> p j c", c=C)
        w1_hi = ctxT_hi[:, 0:E * H]
        w1_lo = ctxT_lo[:, 0:E * H]
        w2_hi = ctx_hi[:, 0:E * H].rearrange("p (e c d) -> p e c d", e=E, d=D)
        w2_lo = ctx_lo[:, 0:E * H].rearrange("p (e c d) -> p e c d", e=E, d=D)
        w_raw = sb("w_raw", [P, W_RING, 2, H])

        ident = sb("ident", [P, P])
        wq_sb = sb("wq_sb", [P, HID])
        wk_sb = sb("wk_sb", [CA, HID])
        wkT = sb("wkT", [HID, CA])
        wv_sb = sb("wv_sb", [CA, HID + 1])
        NROW = E * HC + E
        rows = sb("rows", [NROW, P])
        cols = sb("cols", [P, NROW])
        bq_sb = sb("bq_sb", [P, 1])
        wr_sb = sb("wr_sb", [P, E])
        br_sb = sb("br_sb", [P, E])
        gates = sb("gates", [P, 2])
        tanh_g = sb("tanh_g", [P, 2])
        minus_half = sb("minus_half", [P, NT])
        earlier = sb("earlier", [P, E, E])
        sel = sb("sel", [2 * E, E, P], F32R)

        tok = sb("tok", [P, NT, D])
        norm = sb("norm", [P, NT, D])
        stats = sb("stats", [P, 2, NT, 6])
        mv = sb("mv", [P, 2, NT, 2])
        veps = sb("veps", [P, 2, NT])
        rstd = sb("rstd", [P, 2, NT])
        xT = sb("xT", [P, NTOK])
        qT = sb("qT", [P, MAXN])
        q_f = sb("q_f", [CA, NTOK])
        q_hi = sb("q_hi", [CA, NTOK], F32R)
        q_lo = sb("q_lo", [C, NTOK], F32R)
        pmax = sb("pmax", [P, NT, NMAX])
        nmax = sb("nmax", [P, NT])
        ex = sb("ex", [P, P_RING, 2 * MAXN])
        ex_hi = sb("ex_hi", [P, P_RING, 2 * MAXN], F32R)
        ex_lo = sb("ex_lo", [P, P_RING, 2 * MAXN], F32R)
        ctxT_f = ex[:, :, :].rearrange("p r n -> p (r n)")
        u_sb = sb("u_sb", [CA, MAXN])
        rsum = sb("rsum", [P, NT])
        gsum = sb("gsum", [P, NT])
        xT_hi = sb("xT_hi", [P, NTOK], F32R)
        xT_lo = sb("xT_lo", [P, NTOK], F32R)
        lg = sb("lg", [P, NT, E])
        lmax = sb("lmax", [P, NT])
        ld = sb("ld", [P, NT, E])
        le = sb("le", [P, NT, E])
        cmp_gt = sb("cmp_gt", [P, 3, E, E])
        cmp_eq = sb("cmp_eq", [P, 3, E, E])
        rank = sb("rank", [P, NT, E])
        esum = sb("esum", [P, NT])
        einv = sb("einv", [P, NT])
        picked = sb("picked", [P, NT, E])
        psumw = sb("psumw", [P, NT])
        pinv = sb("pinv", [P, NT])
        routed = sb("routed", [P, NT, E])
        r_hi = sb("r_hi", [P, NT, E], F32R)
        r_cat = sb("r_cat", [P, NT, 2 * E])
        rT = sb("rT", [2 * E, NTOK], F32R)
        r_b = sb("r_b", [P, 2, MAXN])
        y_r = sb("y_r", [P, 2, MAXN])
        acc = sb("acc", [P, NTOK])
        result = norm
        sel_f = acc[0:2 * E, :].rearrange("k (e p) -> k e p", e=E)

        ps = stack.enter_context(nc.psum_tensor("ps", [P, 8, BANK], F32))
        SPAIR = [ps[:, 0:2, :], ps[:, 2:4, :]]
        MPAIR = ps[:, 4:6, :]
        UB = [ps[:, 6, :], ps[:, 7, :]]

        small_in, x_in, w_consts_in = sem("small_in"), sem("x_in"), sem("w_consts_in")
        ctx_in = [sem(f"ctx_in{g}") for g in range(NG)]
        w_in = [sem(f"w_in{r}") for r in range(W_RING)]
        out_done = sem("out_done")
        ident_ready, pad_zeroed, ones_ready, sel_ready, pool_step = sem("ident_ready"), sem("pad_zeroed"), sem("ones_ready"), sem("sel_ready"), sem("pool_step")
        column_ready = sem("column_ready")
        small_turned, small_copied, tanh_ready = sem("small_turned"), sem("small_copied"), sem("tanh_ready")
        rows_turned, rows_copied, psum_ones = sem("rows_turned"), sem("rows_copied"), sem("psum_ones")
        var_ready, rstd_ready, norm_ready = sem("var_ready"), sem("rstd_ready"), sem("norm_ready")
        x_turned, x_copied = sem("x_turned"), sem("x_copied")
        q_made, q_copied, qk_made, qk_copied, q_lo_ready = sem("q_made"), sem("q_copied"), sem("qk_made"), sem("qk_copied"), sem("q_lo_ready")
        ctx_turned, ctxT_hi_ready, ctxT_f_ready, ctxT_lo_ready = sem("ctx_turned"), sem("ctxT_hi_ready"), sem("ctxT_f_ready"), sem("ctxT_lo_ready")
        ctx_hi_ready, ctx_lo_ready = sem("ctx_hi_ready"), sem("ctx_lo_ready")
        max_scores, max_reduced, nmax_ready, max_row, row_ready = sem("max_scores"), sem("max_reduced"), sem("nmax_ready"), sem("max_row"), sem("row_ready")
        scores_ready, ex_ready, lo_ready, ex_used = sem("scores_ready"), sem("ex_ready"), sem("lo_ready"), sem("ex_used")
        u_copied, projected, resid_ready, logits_ready, soft_in, exp_ready = sem("u_copied"), sem("projected"), sem("resid_ready"), sem("logits_ready"), sem("soft_in"), sem("exp_ready")
        xT_lo_ready, routed_ready, r_turned, r_copied = sem("xT_lo_ready"), sem("routed_ready"), sem("r_turned"), sem("r_copied")
        w_hi_ready, w_lo_ready = sem("w_hi_ready"), sem("w_lo_ready")
        h_made, h_ready, h_lo_ready, h_used = sem("h_made"), sem("h_ready"), sem("h_lo_ready"), sem("h_used")
        r_spread, r_b_ready, y_scaled, y_added = sem("r_spread"), sem("r_b_ready"), sem("y_scaled"), sem("y_added")
        y_turned, result_ready = sem("y_turned"), sem("result_ready")
        dve_step = sem("dve_step")

        def width(b):
            return BLOCK_TILES[b] * P

        def tiles(b):
            return slice(FIRST_TILE[b], FIRST_TILE[b] + BLOCK_TILES[b])

        def span(b):
            return slice(FIRST_TILE[b] * P, (FIRST_TILE[b] + BLOCK_TILES[b]) * P)

        Q_STEPS = {(b, step): 3 * (b - 1) + k for b in range(1, NB) for k, step in enumerate(("turn", "q", "qk"))}
        assert max(Q_STEPS.values()) < NG

        def flat(pair):
            return pair.rearrange("p k n -> p (k n)")

        assert POST_ATTENTION["copy_r"] < UNITS

        TURN_UNIT = 14

        assert POST_EXPERTS["copy_r"] <= FU + TURN_UNIT

        def step_at(b, i, name):
            return (POST_ATTENTION if b < NB - 1 else POST_EXPERTS)[name] == i

        def bank_of_hidden(u):
            return ps[:, u % 4, :]

        def ex_pair(buf, slot, chunks, n):
            return buf[:, slot, 0:len(chunks) * n].rearrange("p (k n) -> p k n", n=n)

        def hid(buf, u, n):
            return buf[:, :, :].rearrange("p r n -> p (r n)")[:, (u % H_RING) * MAXN:(u % H_RING) * MAXN + n]

        block = stack.enter_context(nc.Block())

        @block.sync
        def _(sync):
            sync.dma_start(tok[:, :, :], xv).then_inc(x_in, 16)
            sync.dma_start(wk_sb[0:C, :], wk).then_inc(small_in, 16)
            sync.dma_start(wk_sb[C:CA, :], bk.rearrange("(a h) -> a h", a=1)).then_inc(small_in, 16)
            for g in range(NG):
                js = group_chunks(g)
                whole = min(js[-1] + 1, FULL)
                sync.dma_start(raw[:, js[0]:whole, :], ctxv[:, js[0]:whole, :]).then_inc(ctx_in[g], 16)
            sync.wait_ge(pad_zeroed, 1)
            sync.dma_start(raw[0:TAIL, FULL, :], ctx[0, FULL * P:NKEY, :]).then_inc(ctx_in[NG - 1], 16)
            sync.dma_start(wv_sb[0:C, 0:HID], wv).then_inc(w_consts_in, 16)
            sync.dma_start(wv_sb[C:CA, 0:HID], bv.rearrange("(a h) -> a h", a=1)).then_inc(w_consts_in, 16)
            sync.dma_start(wr_sb[:, :], wr).then_inc(w_consts_in, 16)
            sync.dma_start(br_sb[:, :], br.rearrange("(a e) -> a e", a=1).partition_broadcast(P)).then_inc(w_consts_in, 16)
            sync.dma_start(gates[:, 0:1], g_xattn.rearrange("(a e) -> a e", a=1).partition_broadcast(P)).then_inc(w_consts_in, 16)
            sync.dma_start(gates[:, 1:2], g_ffn.rearrange("(a e) -> a e", a=1).partition_broadcast(P)).then_inc(w_consts_in, 16)
            sync.dma_start(rows[0:E * HC, :], b1.rearrange("e (c p) -> (e c) p", p=P)).then_inc(w_consts_in, 16)
            sync.dma_start(rows[E * HC:NROW, :], b2).then_inc(w_consts_in, 16)
            for e in range(E):
                if e >= W_RING:
                    sync.wait_ge(w_lo_ready, e - W_RING + 1)
                slot, landed = w_raw[:, e % W_RING, :, :], w_in[e % W_RING]
                sync.dma_start(slot[:, 0, :], w1[e]).then_inc(landed, 16)
                sync.dma_start(slot[:, 1, :].rearrange("p (c d) -> p c d", d=D),
                               w2[e].rearrange("(c p) d -> p c d", p=P)).then_inc(landed, 16)
            for k, b in enumerate(FFN_ORDER):
                sync.wait_ge(result_ready, k + 1)
                sync.dma_start(outv[:, tiles(b), :], result[:, tiles(b), :]).then_inc(out_done, 16)
            sync.wait_ge(out_done, 16 * NB)

        @block.gpsimd
        def _(pool):
            steps = [0]

            def step(ins):
                steps[0] += 1
                ins.then_inc(pool_step, 1)
                pool.wait_ge(pool_step, steps[0])

            step(nc.gpsimd.memset(ident[:, :], 0.0))
            nc.gpsimd.affine_select(out=ident[:, :], in_=ident[:, :], compare_op=ALU.not_equal, fill=1.0,
                                    base=0, pattern=[[-1, P]], channel_multiplier=1).then_inc(ident_ready, 1)
            nc.gpsimd.memset(raw[:, FULL, :], 0.0).then_inc(pad_zeroed, 1)
            step(nc.gpsimd.memset(minus_half[:, :], -0.5))

            def inverse_deviation(k):
                which, b = k // NB, k % NB
                pool.wait_ge(var_ready, k + 1)
                nc.gpsimd.tensor_tensor(rstd[:, which, tiles(b)], veps[:, which, tiles(b)],
                                        minus_half[:, tiles(b)], ALU.pow).then_inc(rstd_ready, 1)

            inverse_deviation(0)
            last = (NG - 1) * TRANSPOSE_GROUP * P
            pool.wait_ge(rstd_ready, 1)
            step(nc.gpsimd.memset(ctxT_hi[C:CA, last:NKEY].bitcast(F32), 1.0))
            step(nc.gpsimd.memset(ctxT_hi[C:CA, NKEY:NC * P].bitcast(F32), 0.0))
            nc.gpsimd.memset(ch[:, 0:FULL, C].bitcast(F32), 1.0)
            step(nc.gpsimd.memset(ch[:, FULL, C:CA].bitcast(F32), 0.0))
            nc.gpsimd.memset(ch[0:TAIL, FULL, C:CA].bitcast(F32), 1.0).then_inc(ones_ready, 1)
            pool.wait_ge(ones_ready, 1)
            for b in range(1, NB):
                inverse_deviation(b)
            for g in range(NG):
                js = group_chunks(g)
                w = len(js) * P
                pool.wait_ge(ctxT_f_ready, g + 1)
                nc.gpsimd.tensor_tensor(ctxT_lo[0:C, js[0] * P:js[0] * P + w],
                                        ctxT_f[0:C, g % 2 * TRANSPOSE_GROUP * P:g % 2 * TRANSPOSE_GROUP * P + w],
                                        ctxT_hi[0:C, js[0] * P:js[0] * P + w].bitcast(F32),
                                        ALU.subtract).then_inc(ctxT_lo_ready, 1)
            for g in range(NG):
                js = group_chunks(g)
                pool.wait_ge(ctx_hi_ready, g + 1)
                nc.gpsimd.tensor_tensor(cl[:, js[0]:js[-1] + 1, :], raw[:, js[0]:js[-1] + 1, :],
                                        ch[:, js[0]:js[-1] + 1, 0:C].bitcast(F32),
                                        ALU.subtract).then_inc(ctx_lo_ready, 1)
            pool.wait_ge(ctx_lo_ready, NG)
            step(nc.gpsimd.memset(wv_sb[:, HID:HID + 1], 0.0))
            nc.gpsimd.memset(wv_sb[C:CA, HID:HID + 1], 1.0).then_inc(column_ready, 1)
            pool.wait_ge(column_ready, 1)
            nc.gpsimd.memset(earlier[:, :, :], 1.0)
            step(nc.gpsimd.memset(sel_f, 0.0))
            nc.gpsimd.affine_select(out=earlier[:, :, :], in_=earlier[:, :, :], compare_op=ALU.is_gt, fill=0.0,
                                    base=0, pattern=[[1, E], [-1, E]], channel_multiplier=0)
            for half in range(2):
                step(nc.gpsimd.affine_select(out=sel_f, in_=sel_f, compare_op=ALU.not_equal,
                                             fill=1.0, base=-E * half, pattern=[[-1, E], [0, P]],
                                             channel_multiplier=1))
            nc.gpsimd.tensor_copy(sel[:, :, :], sel_f).then_inc(sel_ready, 1)
            for b in range(NB - 1):
                inverse_deviation(NB + b)

            def add_output(k, e):
                b = FFN_ORDER[k]
                if e:
                    pool.wait_ge(y_scaled, k * E + e + 1)
                    if e > 1:
                        pool.wait_ge(y_added, k * (E - 1) + e - 1)
                    nc.gpsimd.tensor_tensor(acc[:, span(b)], acc[:, span(b)], y_r[:, e % 2, 0:width(b)],
                                            ALU.add).then_inc(y_added, 1)

            for e in range(E):
                pool.wait_ge(w_hi_ready, e + 1)
                nc.gpsimd.tensor_tensor(w1_lo[:, e * H:(e + 1) * H], w_raw[:, e % W_RING, 0, :],
                                        w1_hi[:, e * H:(e + 1) * H].bitcast(F32), ALU.subtract)
                nc.gpsimd.tensor_tensor(w2_lo[:, e, :, :].rearrange("p c d -> p (c d)"),
                                        w_raw[:, e % W_RING, 1, :],
                                        w2_hi[:, e, :, :].rearrange("p c d -> p (c d)").bitcast(F32),
                                        ALU.subtract).then_inc(w_lo_ready, 1)
            for k in range(NB):
                for e in range(E):
                    if k == 0 and e == 1:
                        inverse_deviation(2 * NB - 1)
                    add_output(k, e)

        @block.scalar
        def _(act):
            act.dma_start(wq_sb[:, :], wq).then_inc(small_in, 16)
            act.dma_start(bq_sb[:, :], bq.rearrange("(h a) -> h a", a=1)).then_inc(small_in, 16)
            act.preload_act_table(ACT.Exp)
            act.wait_ge(small_turned, 1)
            nc.scalar.copy(wkT[:, :], UB[1][:, 0:CA]).then_inc(small_copied, 1)

            def copy_ctxT(g):
                js = group_chunks(g)
                w = len(js) * P
                rows_ = CA if g + 1 < NG else C
                act.wait_ge(ctx_turned, g + 1)
                if g == 0:
                    act.wait_ge(psum_ones, 1)
                nc.scalar.copy(ctxT_hi[0:rows_, js[0] * P:js[0] * P + w],
                               flat(SPAIR[g % 2])[0:rows_, 0:w]).then_inc(ctxT_hi_ready, 1)
                if g >= 2:
                    act.wait_ge(ctxT_lo_ready, g - 1)
                half = g % 2 * TRANSPOSE_GROUP * P
                nc.scalar.copy(ctxT_f[0:C, half:half + w], flat(SPAIR[g % 2])[0:C, 0:w]).then_inc(ctxT_f_ready, 1)

            def copy_ctx(g):
                js = group_chunks(g)
                act.wait_ge(ctx_in[g], 16 if js[-1] < FULL else 32)
                nc.scalar.copy(ch[:, js[0]:js[-1] + 1, 0:C], raw[:, js[0]:js[-1] + 1, :]).then_inc(ctx_hi_ready, 1)

            def copy_x(b):
                act.wait_ge(x_turned, b + 1)
                nc.scalar.copy(xT[:, span(b)], UB[0][:, 0:width(b)]).then_inc(x_copied, 1)

            def copy_q(b):
                act.wait_ge(q_made, b + 1)
                nc.scalar.activation(qT[:, 0:width(b)], UB[1][:, 0:width(b)], ACT.Identity,
                                     bias=bq_sb[:, :]).then_inc(q_copied, 1)

            def copy_qk(b):
                act.wait_ge(qk_made, b + 1)
                nc.scalar.activation(q_f[:, span(b)], UB[0][0:CA, 0:width(b)], ACT.Copy, scale=SCALE)
                nc.scalar.activation(q_hi[:, span(b)], UB[0][0:CA, 0:width(b)], ACT.Copy,
                                     scale=SCALE).then_inc(qk_copied, 1)

            copy_x(0)
            copy_ctxT(0)
            copy_q(0)
            copy_qk(0)
            copy_ctxT(1)
            for g in range(NG):
                for b in range(1, NB):
                    for name, copy in (("turn", copy_x), ("q", copy_q), ("qk", copy_qk)):
                        if Q_STEPS[b, name] == g:
                            copy(b)
                if g + 2 < NG:
                    copy_ctxT(g + 2)
            for g in range(NG):
                copy_ctx(g)
            act.wait_ge(w_consts_in, 8 * 16)
            nc.scalar.activation(tanh_g[:, :], gates[:, :], ACT.Tanh).then_inc(tanh_ready, 1)
            act.wait_ge(rows_turned, 1)
            nc.scalar.copy(cols[:, :], UB[1][:, 0:NROW]).then_inc(rows_copied, 1)

            def post(b, i):
                n = width(b)
                if step_at(b, i, "u_copy"):
                    act.wait_ge(ex_used, (b + 1) * UNITS)
                    nc.scalar.copy(u_sb[:, 0:n], UB[b % 2][0:CA, 0:n]).then_inc(u_copied, 1)
                if step_at(b, i, "turn"):
                    act.wait_ge(x_turned, NB + b + 1)
                    nc.scalar.copy(xT[:, span(b)], UB[b % 2][:, 0:n])
                    nc.scalar.copy(xT_hi[:, span(b)], UB[b % 2][:, 0:n]).then_inc(x_copied, 1)
                if step_at(b, i, "exp"):
                    act.wait_ge(soft_in, b + 1)
                    nc.scalar.activation(le[:, tiles(b), :], ld[:, tiles(b), :], ACT.Exp).then_inc(exp_ready, 1)
                if step_at(b, i, "copy_r"):
                    act.wait_ge(r_turned, b + 1)
                    nc.scalar.copy(rT[:, span(b)], UB[b % 2][0:2 * E, 0:n]).then_inc(r_copied, 1)

            for b in range(NB):
                n = width(b)
                for i in range(UNITS):
                    u = b * UNITS + i
                    js = unit_chunks(i)
                    act.wait_ge(scores_ready, u + 1)
                    if u == 0:
                        act.wait_ge(ctxT_lo_ready, NG)
                    if u >= P_RING:
                        act.wait_ge(ex_used, u - P_RING + 1)
                        act.wait_ge(lo_ready, u - P_RING + 1)
                    scores = SPAIR[u % 2][:, 0:len(js), 0:n]
                    nc.scalar.activation(ex_pair(ex, u % P_RING, js, n), scores, ACT.Exp)
                    nc.scalar.activation(ex_pair(ex_hi, u % P_RING, js, n), scores, ACT.Exp).then_inc(ex_ready, 1)
                    if b:
                        post(b - 1, i)

            for k, b in enumerate(FFN_ORDER):
                n = width(b)
                for i in range(FU):
                    u = k * FU + i
                    act.wait_ge(h_made, u + 1)
                    if u >= H_RING:
                        act.wait_ge(h_used, u - H_RING + 1)
                        act.wait_ge(h_lo_ready, u - H_RING + 1)
                    else:
                        act.wait_ge(ex_used, NB * UNITS)
                    src = bank_of_hidden(u)[:, 0:n]
                    nc.scalar.activation(hid(ex, u, n), src, ACT.Relu, bias=cols[:, i:i + 1])
                    nc.scalar.activation(hid(ex_hi, u, n), src, ACT.Relu, bias=cols[:, i:i + 1]).then_inc(h_ready, 1)
                    if k < NB - 1:
                        post(NB - 1, u)

        @block.vector
        def _(dve):
            steps = [0]

            def step(ins):
                steps[0] += 1
                ins.then_inc(dve_step, 1)
                dve.wait_ge(dve_step, steps[0])

            def statistics(which, b):
                for t in range(BLOCK_TILES[b]):
                    last = nc.vector.bn_stats(stats[:, which, FIRST_TILE[b] + t, :], tok[:, FIRST_TILE[b] + t, :])
                step(last)
                for t in range(BLOCK_TILES[b]):
                    last = nc.vector.bn_aggr(mv[:, which, FIRST_TILE[b] + t, :], stats[:, which, FIRST_TILE[b] + t, :])
                step(last)
                nc.vector.tensor_scalar(veps[:, which, tiles(b)], mv[:, which, tiles(b), 1], EPS, None,
                                        ALU.add).then_inc(var_ready, 1)

            def normalize(which, b):
                dve.wait_ge(rstd_ready, which * NB + b + 1)
                for t in range(FIRST_TILE[b], FIRST_TILE[b] + BLOCK_TILES[b]):
                    last = nc.vector.tensor_scalar(norm[:, t, :], tok[:, t, :], mv[:, which, t, 0:1],
                                                   rstd[:, which, t:t + 1], ALU.subtract, ALU.mult)
                last.then_inc(norm_ready, 1)

            def split_q(b):
                dve.wait_ge(qk_copied, b + 1)
                nc.vector.tensor_tensor(q_lo[:, span(b)], q_f[0:C, span(b)], q_hi[0:C, span(b)].bitcast(F32),
                                        ALU.subtract).then_inc(q_lo_ready, 1)

            def reduce_max(b, s):
                t, _, w, place = SLOTS[b][s]
                dve.wait_ge(max_scores, SLOTS_BEFORE[b] + s + 1)
                nc.vector.tensor_reduce(pmax[:, FIRST_TILE[b] + t, place:place + 1], MPAIR[:, s % 2, 0:w], AX.X,
                                        ALU.max).then_inc(max_reduced, 1)

            def finish_max(b):
                dve.wait_ge(max_reduced, SLOTS_BEFORE[b] + len(SLOTS[b]))
                nc.vector.tensor_reduce(nmax[:, tiles(b)], pmax[:, tiles(b), :], AX.X, ALU.max,
                                        negate=True).then_inc(nmax_ready, 1)

            def row_max(b):
                dve.wait_ge(max_row, b + 1)
                nc.vector.tensor_tensor(q_hi[C:CA, span(b)], MPAIR[C:CA, 0, 0:width(b)], q_f[C:CA, span(b)],
                                        ALU.add).then_inc(row_ready, 1)

            nc.vector.memset(flat(SPAIR[0])[C:CA, :], 1.0)
            nc.vector.memset(flat(SPAIR[1])[C:CA, :], 1.0).then_inc(psum_ones, 1)
            dve.wait_ge(x_in, 16)
            statistics(0, 0)
            normalize(0, 0)
            for b in range(1, NB):
                statistics(0, b)
                normalize(0, b)
            split_q(0)
            for s in range(len(SLOTS[0])):
                reduce_max(0, s)
            finish_max(0)
            row_max(0)
            for b in range(1, NB):
                split_q(b)

            def post(b, i):
                n, ts = width(b), tiles(b)
                nt = BLOCK_TILES[b]
                bank = UB[b % 2]
                proj = bank[:, 0:nt * (HID + 1)].rearrange("p (t h) -> p t h", h=HID + 1)
                if step_at(b, i, "gate"):
                    dve.wait_ge(projected, b + 1)
                    step(nc.vector.reciprocal(rsum[:, ts], proj[:, :, HID]))
                    dve.wait_ge(tanh_ready, 1)
                    step(nc.vector.tensor_scalar(gsum[:, ts], rsum[:, ts], tanh_g[:, 0:1], None, ALU.mult))
                if step_at(b, i, "residual"):
                    for t in range(nt):
                        ft = FIRST_TILE[b] + t
                        last = nc.vector.scalar_tensor_tensor(out=tok[:, ft, :], in0=proj[:, t, 0:HID],
                                                              scalar=gsum[:, ft:ft + 1], in1=tok[:, ft, :],
                                                              op0=ALU.mult, op1=ALU.add)
                    step(last)
                if step_at(b, i, "stats"):
                    statistics(1, b)
                if step_at(b, i, "normalize"):
                    normalize(1, b)
                if step_at(b, i, "split"):
                    dve.wait_ge(x_copied, NB + b + 1)
                    nc.vector.tensor_tensor(xT_lo[:, span(b)], xT[:, span(b)], xT_hi[:, span(b)].bitcast(F32),
                                            ALU.subtract).then_inc(xT_lo_ready, 1)
                if step_at(b, i, "shift"):
                    dve.wait_ge(logits_ready, b + 1)
                    dve.wait_ge(w_consts_in, 8 * 16)
                    step(nc.vector.tensor_tensor(lg[:, ts, :], bank[:, 0:nt * E].rearrange("p (t e) -> p t e", e=E),
                                                 br_sb[:, :].unsqueeze(1).to_broadcast([P, nt, E]), ALU.add))
                    step(nc.vector.tensor_reduce(lmax[:, ts], lg[:, ts, :], AX.X, ALU.max))
                    nc.vector.tensor_tensor(ld[:, ts, :], lg[:, ts, :],
                                            lmax[:, ts].unsqueeze(2).to_broadcast([P, nt, E]),
                                            ALU.subtract).then_inc(soft_in, 1)
                if step_at(b, i, "compare"):
                    own = lg[:, ts, :].unsqueeze(3).to_broadcast([P, nt, E, E])
                    other = lg[:, ts, :].unsqueeze(2).to_broadcast([P, nt, E, E])
                    nc.vector.tensor_tensor(cmp_gt[:, 0:nt, :, :], other, own, ALU.is_gt)
                    step(nc.vector.tensor_tensor(cmp_eq[:, 0:nt, :, :], other, own, ALU.is_equal))
                if step_at(b, i, "rank"):
                    step(nc.vector.tensor_tensor(cmp_eq[:, 0:nt, :, :], cmp_eq[:, 0:nt, :, :],
                                                 earlier[:, :, :].unsqueeze(1).to_broadcast([P, nt, E, E]),
                                                 ALU.mult))
                    step(nc.vector.tensor_tensor(cmp_gt[:, 0:nt, :, :], cmp_gt[:, 0:nt, :, :],
                                                 cmp_eq[:, 0:nt, :, :], ALU.add))
                    nc.vector.tensor_reduce(rank[:, ts, :], cmp_gt[:, 0:nt, :, :], AX.X, ALU.add)
                if step_at(b, i, "weights"):
                    dve.wait_ge(exp_ready, b + 1)
                    step(nc.vector.tensor_reduce(esum[:, ts], le[:, ts, :], AX.X, ALU.add))
                    step(nc.vector.reciprocal(einv[:, ts], esum[:, ts]))
                    step(nc.vector.tensor_tensor(le[:, ts, :], le[:, ts, :],
                                                 einv[:, ts].unsqueeze(2).to_broadcast([P, nt, E]), ALU.mult))
                if step_at(b, i, "pick"):
                    step(nc.vector.scalar_tensor_tensor(out=picked[:, ts, :], in0=rank[:, ts, :], scalar=2.0,
                                                        in1=le[:, ts, :], op0=ALU.is_lt, op1=ALU.mult))
                    step(nc.vector.tensor_reduce(psumw[:, ts], picked[:, ts, :], AX.X, ALU.add))
                    step(nc.vector.reciprocal(pinv[:, ts], psumw[:, ts]))
                if step_at(b, i, "share"):
                    step(nc.vector.tensor_tensor(routed[:, ts, :], picked[:, ts, :],
                                                 pinv[:, ts].unsqueeze(2).to_broadcast([P, nt, E]), ALU.mult))
                    step(nc.vector.tensor_copy(r_hi[:, ts, :], routed[:, ts, :]))
                    nc.vector.tensor_copy(r_cat[:, ts, 0:E], r_hi[:, ts, :].bitcast(F32))
                    nc.vector.tensor_tensor(r_cat[:, ts, E:2 * E], routed[:, ts, :], r_hi[:, ts, :].bitcast(F32),
                                            ALU.subtract).then_inc(routed_ready, 1)

            def round_weights(e):
                dve.wait_ge(ex_used, (NB - 1) * UNITS + split_unit(e) + 1)
                dve.wait_ge(w_in[e % W_RING], 32 * (e // W_RING + 1))
                nc.vector.tensor_copy(w1_hi[:, e * H:(e + 1) * H], w_raw[:, e % W_RING, 0, :])
                nc.vector.tensor_copy(w2_hi[:, e, :, :].rearrange("p c d -> p (c d)"),
                                      w_raw[:, e % W_RING, 1, :]).then_inc(w_hi_ready, 1)

            for b in range(NB):
                n = width(b)
                for i in range(UNITS):
                    u = b * UNITS + i
                    js = unit_chunks(i)
                    for s in slots_at(b, i):
                        reduce_max(b + 1, s)
                    dve.wait_ge(ex_ready, u + 1)
                    if u >= P_RING:
                        dve.wait_ge(ex_used, u - P_RING + 1)
                    m = len(js) * n
                    nc.vector.tensor_tensor(ex_lo[:, u % P_RING, 0:m], ex[:, u % P_RING, 0:m],
                                            ex_hi[:, u % P_RING, 0:m].bitcast(F32), ALU.subtract).then_inc(lo_ready, 1)
                    for e in range(E):
                        if b == NB - 1 and i == min(split_unit(e) + LAG + 2, UNITS - 1):
                            round_weights(e)
                    if b + 1 < NB and i == MAX_ROW_UNIT - 1:
                        finish_max(b + 1)
                    if b + 1 < NB and i == MAX_ROW_UNIT:
                        row_max(b + 1)
                    if b:
                        post(b - 1, i)

            def spread_row(k, e):
                dve.wait_ge(r_spread, k * E + e + 1)
                if k * E + e >= 2:
                    dve.wait_ge(y_scaled, k * E + e - 1)
                nc.vector.tensor_copy(r_b[:, e % 2, 0:width(FFN_ORDER[k])],
                                      UB[1][:, 0:width(FFN_ORDER[k])]).then_inc(r_b_ready, 1)

            def scale_output(k, e):
                b = FFN_ORDER[k]
                n = width(b)
                dve.wait_ge(h_used, k * FU + (e + 1) * HC)
                dve.wait_ge(r_b_ready, k * E + e + 1)
                if e > 2 or (k and e > 0):
                    before = k * (E - 1) + max(e - 2, 0)
                    if before > 0:
                        dve.wait_ge(y_added, before)
                dst = y_r[:, e % 2, 0:n] if e else acc[:, span(b)]
                nc.vector.scalar_tensor_tensor(out=dst, in0=MPAIR[:, e % 2, 0:n],
                                               scalar=cols[:, E * HC + e:E * HC + e + 1],
                                               in1=r_b[:, e % 2, 0:n], op0=ALU.add, op1=ALU.mult).then_inc(y_scaled, 1)

            def finish_block(k):
                b = FFN_ORDER[k]
                dve.wait_ge(y_turned, k + 1)
                nt = BLOCK_TILES[b]
                src = UB[0][:, 0:nt * P].rearrange("p (t d) -> p t d", d=P)
                nc.vector.scalar_tensor_tensor(out=result[:, tiles(b), :], in0=src, scalar=tanh_g[:, 1:2],
                                               in1=tok[:, tiles(b), :], op0=ALU.mult, op1=ALU.add).then_inc(result_ready, 1)

            for k, b in enumerate(FFN_ORDER):
                n = width(b)
                for i in range(FU):
                    u = k * FU + i
                    e = i // HC
                    if i % HC == 0:
                        spread_row(k, e)
                    dve.wait_ge(h_ready, u + 1)
                    if u >= H_RING:
                        dve.wait_ge(h_used, u - H_RING + 1)
                    nc.vector.tensor_tensor(hid(ex_lo, u, n), hid(ex, u, n), hid(ex_hi, u, n).bitcast(F32),
                                            ALU.subtract).then_inc(h_lo_ready, 1)
                    if i % HC == H_LAG and e > 0:
                        scale_output(k, e - 1)
                    if i == H_LAG and k > 0:
                        scale_output(k - 1, E - 1)
                    if i == TURN_UNIT and k > 0:
                        finish_block(k - 1)
                    if k < NB - 1:
                        post(NB - 1, u)
            scale_output(NB - 1, E - 1)
            finish_block(NB - 1)

        @block.tensor
        def _(pe):
            pe.wait_ge(ident_ready, 1)
            pe.wait_ge(small_in, 4 * 16)
            nc.tensor.transpose(UB[1][:, 0:CA], wk_sb[:, :], ident[0:CA, 0:CA]).then_inc(small_turned, 1)

            def turn_ctx(g, part, parts):
                js = group_chunks(g)
                size = -(-len(js) // parts)
                if part == 0:
                    pe.wait_ge(ctx_in[g], 16 if js[-1] < FULL else 32)
                    if g >= 2:
                        pe.wait_ge(ctxT_f_ready, g - 1)
                for k in range(part * size, min((part + 1) * size, len(js))):
                    ins = nc.tensor.transpose(flat(SPAIR[g % 2])[0:C, k * P:(k + 1) * P], raw[:, js[k], :], ident[:, :])
                    if k == len(js) - 1:
                        ins.then_inc(ctx_turned, 1)

            def turn_x(which, b, bank):
                pe.wait_ge(norm_ready, which * NB + b + 1)
                for t in range(BLOCK_TILES[b]):
                    last = nc.tensor.transpose(bank[:, t * P:(t + 1) * P], norm[:, FIRST_TILE[b] + t, :], ident[:, :])
                last.then_inc(x_turned, 1)

            def make_q(b):
                pe.wait_ge(small_copied, 1)
                pe.wait_ge(x_copied, b + 1)
                nc.tensor.matmul(UB[1][:, 0:width(b)], wq_sb[:, :], xT[:, span(b)], start=True, stop=True).then_inc(q_made, 1)

            def make_qk(b):
                pe.wait_ge(q_copied, b + 1)
                nc.tensor.matmul(UB[0][0:CA, 0:width(b)], wkT[:, :], qT[:, 0:width(b)], start=True,
                                 stop=True).then_inc(qk_made, 1)

            def score_for_max(b, s):
                t, key, w, place = SLOTS[b][s]
                ft = FIRST_TILE[b] + t
                if s >= 2:
                    pe.wait_ge(max_reduced, SLOTS_BEFORE[b] + s - 1)
                elif b:
                    pe.wait_ge(row_ready, b)
                nc.tensor.matmul(MPAIR[:, s % 2, 0:w], q_hi[:, ft * P:(ft + 1) * P], ctxT_hi[0:CA, key:key + w],
                                 start=True, stop=True).then_inc(max_scores, 1)

            def turn_max(b):
                pe.wait_ge(nmax_ready, b + 1)
                for t in range(BLOCK_TILES[b]):
                    ft = FIRST_TILE[b] + t
                    last = nc.tensor.matmul(MPAIR[C:CA, 0, t * P:(t + 1) * P], nmax[:, ft:ft + 1], ident[:, :],
                                            start=True, stop=True)
                last.then_inc(max_row, 1)

            turn_x(0, 0, UB[0])
            turn_ctx(0, 0, 1)
            make_q(0)
            make_qk(0)
            turn_ctx(1, 0, 1)
            pe.wait_ge(qk_copied, 1)
            per_group = TRANSPOSE_GROUP * P // BANK * BLOCK_TILES[0]
            for g in range(NG):
                for b in range(1, NB):
                    if Q_STEPS[b, "turn"] == g:
                        pe.wait_ge(qk_copied, b)
                        turn_x(0, b, UB[0])
                    if Q_STEPS[b, "q"] == g:
                        make_q(b)
                    if Q_STEPS[b, "qk"] == g:
                        make_qk(b)
                pe.wait_ge(ctxT_hi_ready, g + 1)
                if g == NG - 1:
                    pe.wait_ge(ones_ready, 1)
                for s in range(g * per_group, min((g + 1) * per_group, len(SLOTS[0]))):
                    score_for_max(0, s)
                    part = s - g * per_group
                    if g + 2 < NG:
                        turn_ctx(g + 2, part, per_group)
            pe.wait_ge(w_consts_in, 8 * 16)
            pe.wait_ge(qk_copied, NB)
            nc.tensor.transpose(UB[1][:, 0:NROW], rows[:, :], ident[0:NROW, 0:NROW]).then_inc(rows_turned, 1)
            turn_max(0)

            def scores(b, i):
                u = b * UNITS + i
                n = width(b)
                if i == 0:
                    pe.wait_ge(row_ready, b + 1)
                    pe.wait_ge(q_lo_ready, b + 1)
                if b == 0:
                    pe.wait_ge(ctxT_lo_ready, unit_chunks(i)[-1] // TRANSPOSE_GROUP + 1)
                if u < 2:
                    pe.wait_ge(ctxT_f_ready, NG)
                if u >= 2:
                    pe.wait_ge(ex_ready, u - 1)
                for k, j in enumerate(unit_chunks(i)):
                    dst = SPAIR[u % 2][:, k, 0:n]
                    keys = slice(j * P, (j + 1) * P)
                    nc.tensor.matmul(dst, ctxT_hi[0:CA, keys], q_hi[:, span(b)], start=True, stop=False)
                    nc.tensor.matmul(dst, ctxT_hi[0:C, keys], q_lo[:, span(b)], start=False, stop=False)
                    last = nc.tensor.matmul(dst, ctxT_lo[0:C, keys], q_hi[0:C, span(b)], start=False, stop=True)
                last.then_inc(scores_ready, 1)

            def values(b, i):
                u = b * UNITS + i
                n = width(b)
                js = unit_chunks(i)
                dst = UB[b % 2]
                pe.wait_ge(lo_ready, u + 1)
                if b == 0:
                    g = js[-1] // TRANSPOSE_GROUP
                    pe.wait_ge(ctx_lo_ready, g + 1)
                if i == 0 and b >= 2:
                    pe.wait_ge(r_copied, b - 1)
                if i == 0 and b == 1:
                    pe.wait_ge(rows_copied, 1)
                for k, j in enumerate(js):
                    hi = ex_hi[:, u % P_RING, k * n:(k + 1) * n]
                    lo = ex_lo[:, u % P_RING, k * n:(k + 1) * n]
                    nc.tensor.matmul(dst[0:CA, 0:n], ch[:, j, :], hi, start=(j == 0), stop=False)
                    nc.tensor.matmul(dst[0:C, 0:n], cl[:, j, :], hi, start=False, stop=False)
                    last = nc.tensor.matmul(dst[0:CA, 0:n], ch[:, j, :], lo, start=False, stop=(j == NC - 1))
                last.then_inc(ex_used, 1)

            def post(b, i):
                n, nt = width(b), BLOCK_TILES[b]
                bank = UB[b % 2]
                if step_at(b, i, "project"):
                    pe.wait_ge(u_copied, b + 1)
                    pe.wait_ge(column_ready, 1)
                    for t in range(nt):
                        last = nc.tensor.matmul(bank[:, t * (HID + 1):(t + 1) * (HID + 1)], u_sb[:, t * P:(t + 1) * P],
                                                wv_sb[:, :], start=True, stop=True)
                    last.then_inc(projected, 1)
                if step_at(b, i, "turn"):
                    turn_x(1, b, bank)
                if step_at(b, i, "logits"):
                    pe.wait_ge(x_copied, NB + b + 1)
                    for t in range(nt):
                        ft = FIRST_TILE[b] + t
                        last = nc.tensor.matmul(bank[:, t * E:(t + 1) * E], xT[:, ft * P:(ft + 1) * P], wr_sb[:, :],
                                                start=True, stop=True)
                    last.then_inc(logits_ready, 1)
                if step_at(b, i, "turn_r"):
                    pe.wait_ge(routed_ready, b + 1)
                    for t in range(nt):
                        last = nc.tensor.transpose(bank[0:2 * E, t * P:(t + 1) * P], r_cat[:, FIRST_TILE[b] + t, :],
                                                   ident[:, :])
                    last.then_inc(r_turned, 1)

            for v in range(NB * UNITS + LAG):
                b, i = divmod(v, UNITS)
                if b < NB:
                    scores(b, i)
                    for s in slots_at(b, i):
                        score_for_max(b + 1, s)
                    if b + 1 < NB and i == MAX_ROW_UNIT:
                        turn_max(b + 1)
                    if b:
                        post(b - 1, i)
                if v >= LAG:
                    values(*divmod(v - LAG, UNITS))

            def hidden(k, i):
                b, u = FFN_ORDER[k], k * FU + i
                n = width(b)
                e = i // HC
                if i % HC == 0:
                    if k == 0:
                        pe.wait_ge(w_lo_ready, e + 1)
                    if i == 0:
                        pe.wait_ge(xT_lo_ready, b + 1)
                        pe.wait_ge(r_copied, b + 1)
                        pe.wait_ge(sel_ready, 1)
                    if k * E + e >= 1:
                        pe.wait_ge(r_b_ready, k * E + e)
                    if k == 0 and e == 0:
                        pe.wait_ge(x_copied, NB + NB - 1)
                    nc.tensor.matmul(UB[1][:, 0:n], sel[:, e, :], rT[:, span(b)], start=True, stop=True).then_inc(r_spread, 1)
                if u >= 4:
                    pe.wait_ge(h_ready, u - 3)
                dst = bank_of_hidden(u)[:, 0:n]
                rows_ = slice(i * P, (i + 1) * P)
                nc.tensor.matmul(dst, w1_hi[:, rows_], xT_hi[:, span(b)], start=True, stop=False)
                nc.tensor.matmul(dst, w1_hi[:, rows_], xT_lo[:, span(b)], start=False, stop=False)
                nc.tensor.matmul(dst, w1_lo[:, rows_], xT_hi[:, span(b)], start=False, stop=True).then_inc(h_made, 1)

            def expert_out(k, i):
                b, u = FFN_ORDER[k], k * FU + i
                n = width(b)
                e, c = divmod(i, HC)
                pe.wait_ge(h_lo_ready, u + 1)
                if c == 0 and k * E + e >= 2:
                    pe.wait_ge(y_scaled, k * E + e - 1)
                dst = MPAIR[:, e % 2, 0:n]
                hi, lo = hid(ex_hi, u, n), hid(ex_lo, u, n)
                nc.tensor.matmul(dst, w2_hi[:, e, c, :], hi, start=(c == 0), stop=False)
                nc.tensor.matmul(dst, w2_hi[:, e, c, :], lo, start=False, stop=False)
                nc.tensor.matmul(dst, w2_lo[:, e, c, :], hi, start=False, stop=(c == HC - 1)).then_inc(h_used, 1)

            def turn_output(k):
                b = FFN_ORDER[k]
                pe.wait_ge(y_added, (k + 1) * (E - 1))
                pe.wait_ge(r_copied, NB)
                if k:
                    pe.wait_ge(result_ready, k)
                for t in range(BLOCK_TILES[b]):
                    ft = FIRST_TILE[b] + t
                    last = nc.tensor.transpose(UB[0][:, t * P:(t + 1) * P], acc[:, ft * P:(ft + 1) * P], ident[:, :])
                last.then_inc(y_turned, 1)

            for v in range(NB * FU + H_LAG):
                k, i = divmod(v, FU)
                if k < NB:
                    hidden(k, i)
                    if k < NB - 1:
                        post(NB - 1, v)
                    if k > 0 and i == TURN_UNIT:
                        turn_output(k - 1)
                if v >= H_LAG:
                    expert_out(*divmod(v - H_LAG, FU))
            turn_output(NB - 1)


_INS = ['x', 'ctx_768', 'g_xattn', 'g_ffn', 'L0_xattn_Wq', 'L0_xattn_bq', 'L0_xattn_Wk', 'L0_xattn_bk',
        'L0_xattn_Wv', 'L0_xattn_bv', 'L0_ffn_W1', 'L0_ffn_b1', 'L0_ffn_W2', 'L0_ffn_b2', 'L0_ffn_Wr',
        'L0_ffn_br']
_OUTS = [((1, 1024, 128), 'float32')]


def kernel(**inputs):
    import numpy as _np
    import concourse.bacc as _bacc
    from concourse import mybir as _mybir
    from concourse.bass_utils import run_bass_kernel_spmd as _run

    nc = _bacc.Bacc("TRN2", target_bir_lowering=False, num_devices=1)
    arrays, args = {}, []
    for name in _INS:
        a = _np.ascontiguousarray(inputs[name])
        arrays[f"in_{name}_dram"] = a
        args.append(nc.dram_tensor(f"in_{name}_dram", a.shape, _mybir.dt.from_np(a.dtype), kind="ExternalInput").ap())
    for i, (shape, dtype) in enumerate(_OUTS):
        dt = _mybir.dt.from_np(_np.dtype(dtype))
        args.append(nc.dram_tensor(f"out_{i}_dram", shape, dt, kind="ExternalOutput").ap())
    attention_experts(nc, *args)
    r = _run(nc, [arrays], core_ids=[0])
    got = tuple(r.results[0][f"out_{i}_dram"] for i in range(len(_OUTS)))
    return got[0]
```

```python
from contextlib import ExitStack

import concourse.bass as bass
from concourse import mybir

F32 = mybir.dt.float32
F32R = mybir.dt.float32r
ALU = mybir.AluOpType
ACT = mybir.ActivationFunctionType
AX = mybir.AxisListType

P = 128
BANK = 512
BLOCK_TILES = [2, 3, 3]
NB = len(BLOCK_TILES)
FIRST_TILE = [sum(BLOCK_TILES[:b]) for b in range(NB)]
SPANS = 2
TRANSPOSE_GROUP = 8
LAG = 2
P_RING = 3
H_LAG = 3
H_RING = 4
W_RING = 2
WARM_UP = 18
EPS = 1e-5

STEPS = ["u_copy", "project", "gate", "residual", "stats", "normalize", "turn", "split", "logits", "shift",
         "compare", "exp", "rank", "weights", "pick", "share", "turn_r", "copy_r"]
POST_ATTENTION = dict(zip(STEPS, [3, 5, 5, 6, 7, 9, 12, 13, 14, 15, 16, 17, 17, 18, 19, 20, 23, 24]))
POST_EXPERTS = dict(zip(STEPS, [2, 4, 5, 6, 7, 9, 12, 13, 14, 15, 16, 18, 18, 20, 22, 24, 27, 28]))


def attention_experts(nc, x, ctx, g_xattn, g_ffn, wq, bq, wk, bk, wv, bv, w1, b1, w2, b2, wr, br, out):
    _, NTOK, D = x.shape
    _, NKEY, C = ctx.shape
    HID = wq.shape[1]
    E, _, H = w1.shape
    NT = NTOK // P
    FULL = NKEY // P
    TAIL = NKEY - FULL * P
    NC = FULL + 1
    CA = C + 1
    NG = -(-NC // TRANSPOSE_GROUP)
    UNITS = -(-NC // 2)
    HC = H // P
    FU = E * HC
    SPAN_TILES = NT // SPANS
    SPAN = SPAN_TILES * P
    SCALE = float(HID) ** -0.5
    MAXN = max(BLOCK_TILES) * P
    assert D == P and HID == P and sum(BLOCK_TILES) == NT and TAIL > 0 and C == 96 and SPAN <= BANK
    BLOCKS_FOR = [NB - 1 if (s + 1) * SPAN_TILES <= FIRST_TILE[-1] else NB for s in range(SPANS)]
    assert BLOCKS_FOR == [NB - 1, NB]

    xv = x.rearrange("a (p t) d -> p (a t) d", t=NT)
    outv = out.rearrange("a (p t) d -> p (a t) d", t=NT)
    ctxv = ctx[0, 0:FULL * P, :].rearrange("(p j) c -> p j c", j=FULL)

    def group_chunks(g):
        return range(g * TRANSPOSE_GROUP, min((g + 1) * TRANSPOSE_GROUP, NC))

    def unit_chunks(i):
        return range(2 * i, min(2 * i + 2, NC))

    NMAX = -(-NKEY // BANK)
    SLOTS = [[(t, w * BANK, min(BANK, NKEY - w * BANK), w) for w in range(NMAX) for t in range(n)]
             for n in BLOCK_TILES]
    SLOTS_BEFORE = [sum(len(s) for s in SLOTS[:b]) for b in range(NB)]
    MAX_ROW_UNIT = UNITS - 2

    def slots_at(b, i):
        if b + 1 == NB or i >= MAX_ROW_UNIT - 2:
            return []
        n = len(SLOTS[b + 1])
        return range(i * n // (MAX_ROW_UNIT - 2), (i + 1) * n // (MAX_ROW_UNIT - 2))

    def split_unit(e):
        last_chunk = ((e + 1) * H - 1) // C
        return last_chunk // 2

    with ExitStack() as stack:
        def sb(name, shape, dt=F32):
            return stack.enter_context(nc.sbuf_tensor(name, shape, dt))

        def sem(name):
            return stack.enter_context(nc.semaphore(name))

        raw = sb("raw", [P, NC, C])
        ctx_hi = sb("ctx_hi", [P, NC * CA], F32R)
        ctx_lo = sb("ctx_lo", [P, NC * C], F32R)
        ctxT_hi = sb("ctxT_hi", [P, NC * P], F32R)
        ctxT_lo = sb("ctxT_lo", [P, NC * P], F32R)
        ch = ctx_hi[:, :].rearrange("p (j c) -> p j c", c=CA)
        cl = ctx_lo[:, :].rearrange("p (j c) -> p j c", c=C)
        w1_hi = ctxT_hi[:, 0:E * H]
        w1_lo = ctxT_lo[:, 0:E * H]
        w2_hi = ctx_hi[:, 0:E * H].rearrange("p (e c d) -> p e c d", e=E, d=D)
        w2_lo = ctx_lo[:, 0:E * H].rearrange("p (e c d) -> p e c d", e=E, d=D)
        w_raw = sb("w_raw", [P, W_RING, 2, H])

        ident = sb("ident", [P, P])
        wq_sb = sb("wq_sb", [P, HID])
        wk_sb = sb("wk_sb", [CA, HID])
        wkT = sb("wkT", [HID, CA])
        wv_sb = sb("wv_sb", [CA, HID + 1])
        NROW = E * HC + E
        rows = sb("rows", [NROW, P])
        cols = sb("cols", [P, NROW])
        bq_sb = sb("bq_sb", [P, 1])
        wr_sb = sb("wr_sb", [P, E])
        br_sb = sb("br_sb", [P, E])
        gates = sb("gates", [P, 2])
        tanh_g = sb("tanh_g", [P, 2])
        minus_half = sb("minus_half", [P, NT])
        earlier = sb("earlier", [P, E, E])

        tok = sb("tok", [P, NT, D])
        norm = sb("norm", [P, NT, D])
        stats = sb("stats", [P, 2, NT, 6])
        mv = sb("mv", [P, 2, NT, 2])
        veps = sb("veps", [P, 2, NT])
        rstd = sb("rstd", [P, 2, NT])
        xT = sb("xT", [P, NTOK])
        qT = sb("qT", [P, MAXN])
        q_f = sb("q_f", [CA, NTOK])
        q_hi = sb("q_hi", [CA, NTOK], F32R)
        q_lo = sb("q_lo", [C, NTOK], F32R)
        pmax = sb("pmax", [P, NT, NMAX])
        nmax = sb("nmax", [P, NT])
        ex = sb("ex", [P, P_RING, 2 * MAXN])
        ex_hi = sb("ex_hi", [P, P_RING, 2 * MAXN], F32R)
        ex_lo = sb("ex_lo", [P, P_RING, 2 * MAXN], F32R)
        u_sb = sb("u_sb", [CA, MAXN])
        rsum = sb("rsum", [P, NT])
        gsum = sb("gsum", [P, NT])
        xT_hi = sb("xT_hi", [P, NTOK], F32R)
        xT_lo = sb("xT_lo", [P, NTOK], F32R)
        lg = sb("lg", [P, NT, E])
        lmax = sb("lmax", [P, NT])
        ld = sb("ld", [P, NT, E])
        le = sb("le", [P, NT, E])
        cmp_gt = sb("cmp_gt", [P, 3, E, E])
        cmp_eq = sb("cmp_eq", [P, 3, E, E])
        rank = sb("rank", [P, NT, E])
        esum = sb("esum", [P, NT])
        einv = sb("einv", [P, NT])
        picked = sb("picked", [P, NT, E])
        psumw = sb("psumw", [P, NT])
        pinv = sb("pinv", [P, NT])
        routed = sb("routed", [P, NT, E])
        rT = sb("rT", [E, NTOK])
        r_b = sb("r_b", [P, 2, SPAN])
        y_r = sb("y_r", [P, 2, SPAN])
        acc = sb("acc", [P, NTOK])
        result = norm
        ctxT_f = [w_raw[:, 0, :, :].rearrange("p k n -> p (k n)"), w_raw[:, 1, :, :].rearrange("p k n -> p (k n)"),
                  acc, y_r[:, :, :].rearrange("p k n -> p (k n)"), r_b[:, :, :].rearrange("p k n -> p (k n)")]
        assert min(2 * H, NTOK, 2 * SPAN) >= TRANSPOSE_GROUP * P and W_RING == 2
        r_dram = nc.dram_tensor("routing", [E, NTOK], F32).ap()

        ps = stack.enter_context(nc.psum_tensor("ps", [P, 8, BANK], F32))
        SPAIR = [ps[:, 0:2, :], ps[:, 2:4, :]]
        MPAIR = ps[:, 4:6, :]
        UB = [ps[:, 6, :], ps[:, 7, :]]

        small_in, x_in, w_consts_in = sem("small_in"), sem("x_in"), sem("w_consts_in")
        x_later_in = sem("x_later_in")
        ctx_in = [sem(f"ctx_in{g}") for g in range(NG)]
        w_in = [sem(f"w_in{r}") for r in range(W_RING)]
        out_done = sem("out_done")
        ident_ready, pad_zeroed, ones_ready, earlier_ready, pool_step = sem("ident_ready"), sem("pad_zeroed"), sem("ones_ready"), sem("earlier_ready"), sem("pool_step")
        column_ready = sem("column_ready")
        small_turned, small_copied, tanh_ready = sem("small_turned"), sem("small_copied"), sem("tanh_ready")
        rows_turned, rows_copied, psum_ones = sem("rows_turned"), sem("rows_copied"), sem("psum_ones")
        var_ready, rstd_ready, norm_ready = sem("var_ready"), sem("rstd_ready"), sem("norm_ready")
        x_turned, x_copied = sem("x_turned"), sem("x_copied")
        q_made, q_copied, qk_made, qk_copied, q_lo_ready = sem("q_made"), sem("q_copied"), sem("qk_made"), sem("qk_copied"), sem("q_lo_ready")
        ctx_turned, ctxT_hi_ready, ctxT_f_ready, ctxT_lo_ready = sem("ctx_turned"), sem("ctxT_hi_ready"), sem("ctxT_f_ready"), sem("ctxT_lo_ready")
        ctx_hi_ready, ctx_lo_ready = sem("ctx_hi_ready"), sem("ctx_lo_ready")
        q_hi_ready = sem("q_hi_ready")
        max_scores, max_reduced, nmax_ready, max_row, row_ready = sem("max_scores"), sem("max_reduced"), sem("nmax_ready"), sem("max_row"), sem("row_ready")
        scores_ready, ex_ready, lo_ready, ex_used = sem("scores_ready"), sem("ex_ready"), sem("lo_ready"), sem("ex_used")
        u_copied, projected, logits_ready, soft_in, exp_ready = sem("u_copied"), sem("projected"), sem("logits_ready"), sem("soft_in"), sem("exp_ready")
        xT_lo_ready, routed_ready, r_turned, r_copied = sem("xT_lo_ready"), sem("routed_ready"), sem("r_turned"), sem("r_copied")
        w_hi_ready, w_lo_ready = sem("w_hi_ready"), sem("w_lo_ready")
        h_made, h_ready, h_lo_ready, h_used = sem("h_made"), sem("h_ready"), sem("h_lo_ready"), sem("h_used")
        r_stored, y_scaled, y_added = sem("r_stored"), sem("y_scaled"), sem("y_added")
        r_b_in = [sem("r_b_in0"), sem("r_b_in1")]
        sum_turned, y_turned, result_ready = sem("sum_turned"), sem("y_turned"), sem("result_ready")
        dve_step = sem("dve_step")

        def width(b):
            return BLOCK_TILES[b] * P

        def tiles(b):
            return slice(FIRST_TILE[b], FIRST_TILE[b] + BLOCK_TILES[b])

        def span(b):
            return slice(FIRST_TILE[b] * P, (FIRST_TILE[b] + BLOCK_TILES[b]) * P)

        Q_STEPS = {(b, step): 3 * (b - 1) + k for b in range(1, NB) for k, step in enumerate(("turn", "q", "qk"))}
        assert max(Q_STEPS.values()) < NG

        def flat(pair):
            return pair.rearrange("p k n -> p (k n)")

        assert POST_ATTENTION["copy_r"] < UNITS

        TURN_UNIT = 8
        assert POST_EXPERTS["copy_r"] < FU

        def half_tiles(k):
            return slice(k * SPAN_TILES, (k + 1) * SPAN_TILES)

        END_PARTS = 2
        END_TILES = SPAN_TILES // END_PARTS

        def last_tiles(part):
            start = (SPANS - 1) * SPAN_TILES + part * END_TILES
            return slice(start, start + END_TILES)

        def half(k):
            return slice(k * SPAN, (k + 1) * SPAN)

        def step_at(b, i, name):
            return (POST_ATTENTION if b < NB - 1 else POST_EXPERTS)[name] == i

        def bank_of_hidden(u):
            return ps[:, u % 4, :]

        def ex_pair(buf, slot, chunks, n):
            return buf[:, slot, 0:len(chunks) * n].rearrange("p (k n) -> p k n", n=n)

        def hid(buf, u):
            return buf[:, :, :].rearrange("p r n -> p (r n)")[:, (u % H_RING) * SPAN:(u % H_RING + 1) * SPAN]

        EARLY_CTX = 5

        def ring_left(u):
            first, last = u * SPAN // (2 * MAXN), ((u + 1) * SPAN - 1) // (2 * MAXN)
            return max(v for v in range(NB * UNITS) if first <= v % P_RING <= last) + 1

        EARLY_HIDDEN = 2
        assert EARLY_HIDDEN == LAG and NB * UNITS % 2 == 0

        block = stack.enter_context(nc.Block())

        @block.sync
        def _(sync):
            sync.dma_start(tok[:, tiles(0), :], xv[:, tiles(0), :]).then_inc(x_in, 16)
            sync.dma_start(wk_sb[0:C, :], wk).then_inc(small_in, 16)
            sync.dma_start(wk_sb[C:CA, :], bk.rearrange("(a h) -> a h", a=1)).then_inc(small_in, 16)
            for g in range(NG):
                js = group_chunks(g)
                whole = min(js[-1] + 1, FULL)
                sync.dma_start(raw[:, js[0]:whole, :], ctxv[:, js[0]:whole, :]).then_inc(ctx_in[g], 16)
                if g == 0:
                    later = slice(BLOCK_TILES[0], NT)
                    sync.dma_start(tok[:, later, :], xv[:, later, :]).then_inc(x_later_in, 16)
            sync.wait_ge(pad_zeroed, 1)
            sync.dma_start(raw[0:TAIL, FULL, :], ctx[0, FULL * P:NKEY, :]).then_inc(ctx_in[NG - 1], 16)
            sync.dma_start(wv_sb[0:C, 0:HID], wv).then_inc(w_consts_in, 16)
            sync.dma_start(wv_sb[C:CA, 0:HID], bv.rearrange("(a h) -> a h", a=1)).then_inc(w_consts_in, 16)
            sync.dma_start(wr_sb[:, :], wr).then_inc(w_consts_in, 16)
            sync.dma_start(br_sb[:, :], br.rearrange("(a e) -> a e", a=1).partition_broadcast(P)).then_inc(w_consts_in, 16)
            sync.dma_start(gates[:, 0:1], g_xattn.rearrange("(a e) -> a e", a=1).partition_broadcast(P)).then_inc(w_consts_in, 16)
            sync.dma_start(gates[:, 1:2], g_ffn.rearrange("(a e) -> a e", a=1).partition_broadcast(P)).then_inc(w_consts_in, 16)
            sync.dma_start(rows[0:E * HC, :], b1.rearrange("e (c p) -> (e c) p", p=P)).then_inc(w_consts_in, 16)
            sync.dma_start(rows[E * HC:NROW, :], b2).then_inc(w_consts_in, 16)
            sync.wait_ge(ctxT_lo_ready, NG)
            for e in range(E):
                if e >= W_RING:
                    sync.wait_ge(w_lo_ready, e - W_RING + 1)
                slot, landed = w_raw[:, e % W_RING, :, :], w_in[e % W_RING]
                sync.dma_start(slot[:, 0, :], w1[e]).then_inc(landed, 16)
                sync.dma_start(slot[:, 1, :].rearrange("p (c d) -> p c d", d=D),
                               w2[e].rearrange("(c p) d -> p c d", p=P)).then_inc(landed, 16)

            def fetch_routing(k, e):
                sync.wait_ge(r_stored, 16 * BLOCKS_FOR[k])
                if k * E + e >= 2:
                    sync.wait_ge(y_scaled, k * E + e - 1)
                row = r_dram[e:e + 1, half(k)].partition_broadcast(P).rearrange("p a n -> p (a n)")
                sync.dma_start(r_b[:, e % 2, :], row).then_inc(r_b_in[e % 2], 16)

            for k in range(SPANS):
                for e in range(E):
                    fetch_routing(k, e)
                    if k and e == TURN_UNIT // HC:
                        sync.wait_ge(result_ready, k)
                        sync.dma_start(outv[:, half_tiles(k - 1), :], result[:, half_tiles(k - 1), :]).then_inc(out_done, 16)
            sync.wait_ge(result_ready, SPANS)
            sync.dma_start(outv[:, last_tiles(0), :], result[:, last_tiles(0), :]).then_inc(out_done, 16)
            sync.wait_ge(out_done, 16 * (SPANS + 1))

        @block.gpsimd
        def _(pool):
            steps = [0]

            def step(ins):
                steps[0] += 1
                ins.then_inc(pool_step, 1)
                pool.wait_ge(pool_step, steps[0])

            step(nc.gpsimd.memset(ident[:, :], 0.0))
            nc.gpsimd.affine_select(out=ident[:, :], in_=ident[:, :], compare_op=ALU.not_equal, fill=1.0,
                                    base=0, pattern=[[-1, P]], channel_multiplier=1).then_inc(ident_ready, 1)
            nc.gpsimd.memset(raw[:, FULL, :], 0.0).then_inc(pad_zeroed, 1)
            step(nc.gpsimd.memset(minus_half[:, :], -0.5))

            def inverse_deviation(k):
                which, b = k // NB, k % NB
                pool.wait_ge(var_ready, k + 1)
                nc.gpsimd.tensor_tensor(rstd[:, which, tiles(b)], veps[:, which, tiles(b)],
                                        minus_half[:, tiles(b)], ALU.pow).then_inc(rstd_ready, 1)

            inverse_deviation(0)
            last = (NG - 1) * TRANSPOSE_GROUP * P
            pool.wait_ge(rstd_ready, 1)
            step(nc.gpsimd.memset(ctxT_hi[C:CA, last:NKEY].bitcast(F32), 1.0))
            step(nc.gpsimd.memset(ctxT_hi[C:CA, NKEY:NC * P].bitcast(F32), 0.0))
            nc.gpsimd.memset(ch[:, 0:FULL, C].bitcast(F32), 1.0)
            step(nc.gpsimd.memset(ch[:, FULL, C:CA].bitcast(F32), 0.0))
            nc.gpsimd.memset(ch[0:TAIL, FULL, C:CA].bitcast(F32), 1.0).then_inc(ones_ready, 1)
            pool.wait_ge(ones_ready, 1)
            for b in range(1, NB):
                inverse_deviation(b)

            def split_ctxT(g):
                js = group_chunks(g)
                w = len(js) * P
                pool.wait_ge(ctxT_f_ready, g + 1)
                nc.gpsimd.tensor_tensor(ctxT_lo[0:C, js[0] * P:js[0] * P + w], ctxT_f[g % len(ctxT_f)][0:C, 0:w],
                                        ctxT_hi[0:C, js[0] * P:js[0] * P + w].bitcast(F32),
                                        ALU.subtract).then_inc(ctxT_lo_ready, 1)

            def split_ctx(g):
                js = group_chunks(g)
                pool.wait_ge(ctx_hi_ready, g + 1)
                nc.gpsimd.tensor_tensor(cl[:, js[0]:js[-1] + 1, :], raw[:, js[0]:js[-1] + 1, :],
                                        ch[:, js[0]:js[-1] + 1, 0:C].bitcast(F32),
                                        ALU.subtract).then_inc(ctx_lo_ready, 1)

            for g in range(NG):
                split_ctxT(g)
                if g >= EARLY_CTX:
                    split_ctx(g - EARLY_CTX)
            for g in range(NG - EARLY_CTX, NG):
                split_ctx(g)
            pool.wait_ge(ctx_lo_ready, NG)
            step(nc.gpsimd.memset(wv_sb[:, HID:HID + 1], 0.0))
            nc.gpsimd.memset(wv_sb[C:CA, HID:HID + 1], 1.0).then_inc(column_ready, 1)
            pool.wait_ge(column_ready, 1)
            step(nc.gpsimd.memset(earlier[:, :, :], 1.0))
            nc.gpsimd.affine_select(out=earlier[:, :, :], in_=earlier[:, :, :], compare_op=ALU.is_gt, fill=0.0,
                                    base=0, pattern=[[1, E], [-1, E]], channel_multiplier=0).then_inc(earlier_ready, 1)
            for b in range(NB - 1):
                inverse_deviation(NB + b)

            def add_output(k, e):
                if e:
                    pool.wait_ge(y_scaled, k * E + e + 1)
                    if e > 1:
                        pool.wait_ge(y_added, k * (E - 1) + e - 1)
                    nc.gpsimd.tensor_tensor(acc[:, half(k)], acc[:, half(k)], y_r[:, e % 2, :],
                                            ALU.add).then_inc(y_added, 1)

            for e in range(E):
                pool.wait_ge(w_hi_ready, e + 1)
                nc.gpsimd.tensor_tensor(w1_lo[:, e * H:(e + 1) * H], w_raw[:, e % W_RING, 0, :],
                                        w1_hi[:, e * H:(e + 1) * H].bitcast(F32), ALU.subtract)
                nc.gpsimd.tensor_tensor(w2_lo[:, e, :, :].rearrange("p c d -> p (c d)"),
                                        w_raw[:, e % W_RING, 1, :],
                                        w2_hi[:, e, :, :].rearrange("p c d -> p (c d)").bitcast(F32),
                                        ALU.subtract).then_inc(w_lo_ready, 1)
            for k in range(SPANS):
                for e in range(E if k < SPANS - 1 else E - 2):
                    if k == 0 and e == 1:
                        inverse_deviation(2 * NB - 1)
                    add_output(k, e)

        @block.scalar
        def _(act):
            act.dma_start(wq_sb[:, :], wq).then_inc(small_in, 16)
            act.dma_start(bq_sb[:, :], bq.rearrange("(h a) -> h a", a=1)).then_inc(small_in, 16)
            act.preload_act_table(ACT.Exp)
            act.wait_ge(small_turned, 1)
            nc.scalar.copy(wkT[:, :], UB[1][:, 0:CA]).then_inc(small_copied, 1)

            def copy_ctxT(g):
                copy_ctxT_hi(g)
                copy_ctxT_whole(g)

            def copy_ctxT_hi(g):
                js = group_chunks(g)
                w = len(js) * P
                rows_ = CA if g + 1 < NG else C
                act.wait_ge(ctx_turned, g + 1)
                if g == 0:
                    act.wait_ge(psum_ones, 1)
                nc.scalar.copy(ctxT_hi[0:rows_, js[0] * P:js[0] * P + w],
                               flat(SPAIR[g % 2])[0:rows_, 0:w]).then_inc(ctxT_hi_ready, 1)

            def copy_ctxT_whole(g):
                w = len(group_chunks(g)) * P
                if g >= len(ctxT_f):
                    act.wait_ge(ctxT_lo_ready, g - len(ctxT_f) + 1)
                nc.scalar.copy(ctxT_f[g % len(ctxT_f)][0:C, 0:w], flat(SPAIR[g % 2])[0:C, 0:w]).then_inc(ctxT_f_ready, 1)

            def copy_ctx(g):
                js = group_chunks(g)
                act.wait_ge(ctx_in[g], 16 if js[-1] < FULL else 32)
                nc.scalar.copy(ch[:, js[0]:js[-1] + 1, 0:C], raw[:, js[0]:js[-1] + 1, :]).then_inc(ctx_hi_ready, 1)

            def copy_x(b):
                act.wait_ge(x_turned, b + 1)
                nc.scalar.copy(xT[:, span(b)], UB[0][:, 0:width(b)]).then_inc(x_copied, 1)

            def copy_q(b):
                act.wait_ge(q_made, b + 1)
                nc.scalar.activation(qT[:, 0:width(b)], UB[1][:, 0:width(b)], ACT.Identity,
                                     bias=bq_sb[:, :]).then_inc(q_copied, 1)

            def copy_qk(b):
                act.wait_ge(qk_made, b + 1)
                nc.scalar.activation(q_hi[:, span(b)], UB[0][0:CA, 0:width(b)], ACT.Copy,
                                     scale=SCALE).then_inc(q_hi_ready, 1)
                nc.scalar.activation(q_f[:, span(b)], UB[0][0:CA, 0:width(b)], ACT.Copy,
                                     scale=SCALE).then_inc(qk_copied, 1)

            copy_x(0)
            copy_q(0)
            copy_ctxT_hi(0)
            copy_qk(0)
            copy_ctxT_whole(0)
            copy_ctxT(1)
            for g in range(NG):
                for b in range(1, NB):
                    for name, copy in (("turn", copy_x), ("q", copy_q), ("qk", copy_qk)):
                        if Q_STEPS[b, name] == g:
                            copy(b)
                if g + 2 < NG:
                    copy_ctxT(g + 2)
                    if g + 2 >= EARLY_CTX:
                        copy_ctx(g + 2 - EARLY_CTX)
            for g in range(NG - EARLY_CTX, NG):
                copy_ctx(g)
            act.wait_ge(w_consts_in, 8 * 16)
            nc.scalar.activation(tanh_g[:, :], gates[:, :], ACT.Tanh).then_inc(tanh_ready, 1)
            act.wait_ge(rows_turned, 1)
            nc.scalar.copy(cols[:, :], UB[1][:, 0:NROW]).then_inc(rows_copied, 1)

            def post(b, i):
                n = width(b)
                if step_at(b, i, "u_copy"):
                    act.wait_ge(ex_used, (b + 1) * UNITS)
                    nc.scalar.copy(u_sb[:, 0:n], UB[b % 2][0:CA, 0:n]).then_inc(u_copied, 1)
                if step_at(b, i, "turn"):
                    act.wait_ge(x_turned, NB + b + 1)
                    nc.scalar.copy(xT[:, span(b)], UB[b % 2][:, 0:n])
                    nc.scalar.copy(xT_hi[:, span(b)], UB[b % 2][:, 0:n]).then_inc(x_copied, 1)
                if step_at(b, i, "exp"):
                    act.wait_ge(soft_in, b + 1)
                    nc.scalar.activation(le[:, tiles(b), :], ld[:, tiles(b), :], ACT.Exp).then_inc(exp_ready, 1)
                if step_at(b, i, "copy_r"):
                    act.wait_ge(r_turned, b + 1)
                    nc.scalar.copy(rT[:, span(b)], UB[b % 2][0:E, 0:n]).then_inc(r_copied, 1)
                    act.wait_ge(r_copied, b + 1)
                    act.dma_start(r_dram[:, span(b)], rT[:, span(b)]).then_inc(r_stored, 16)

            for b in range(NB):
                n = width(b)
                for i in range(UNITS):
                    u = b * UNITS + i
                    js = unit_chunks(i)
                    act.wait_ge(scores_ready, u + 1)
                    if u >= P_RING:
                        act.wait_ge(ex_used, u - P_RING + 1)
                        act.wait_ge(lo_ready, u - P_RING + 1)
                    scores = SPAIR[u % 2][:, 0:len(js), 0:n]
                    nc.scalar.activation(ex_pair(ex, u % P_RING, js, n), scores, ACT.Exp)
                    nc.scalar.activation(ex_pair(ex_hi, u % P_RING, js, n), scores, ACT.Exp).then_inc(ex_ready, 1)
                    if b:
                        post(b - 1, i)

            for k in range(SPANS):
                for i in range(FU):
                    u = k * FU + i
                    act.wait_ge(h_made, u + 1)
                    if u >= H_RING:
                        act.wait_ge(h_used, u - H_RING + 1)
                        act.wait_ge(h_lo_ready, u - H_RING + 1)
                    else:
                        act.wait_ge(ex_used, ring_left(u))
                    src = bank_of_hidden(u)[:, 0:SPAN]
                    nc.scalar.activation(hid(ex, u), src, ACT.Relu, bias=cols[:, i:i + 1])
                    nc.scalar.activation(hid(ex_hi, u), src, ACT.Relu, bias=cols[:, i:i + 1]).then_inc(h_ready, 1)
                    if k == 0:
                        post(NB - 1, u)
            act.wait_ge(result_ready, SPANS - 1 + END_PARTS)
            act.dma_start(outv[:, last_tiles(1), :], result[:, last_tiles(1), :]).then_inc(out_done, 16)

        @block.vector
        def _(dve):
            steps = [0]

            def step(ins):
                steps[0] += 1
                ins.then_inc(dve_step, 1)
                dve.wait_ge(dve_step, steps[0])

            def statistics(which, b):
                for t in range(BLOCK_TILES[b]):
                    last = nc.vector.bn_stats(stats[:, which, FIRST_TILE[b] + t, :], tok[:, FIRST_TILE[b] + t, :])
                step(last)
                for t in range(BLOCK_TILES[b]):
                    last = nc.vector.bn_aggr(mv[:, which, FIRST_TILE[b] + t, :], stats[:, which, FIRST_TILE[b] + t, :])
                step(last)
                nc.vector.tensor_scalar(veps[:, which, tiles(b)], mv[:, which, tiles(b), 1], EPS, None,
                                        ALU.add).then_inc(var_ready, 1)

            def normalize(which, b):
                dve.wait_ge(rstd_ready, which * NB + b + 1)
                for t in range(FIRST_TILE[b], FIRST_TILE[b] + BLOCK_TILES[b]):
                    last = nc.vector.tensor_scalar(norm[:, t, :], tok[:, t, :], mv[:, which, t, 0:1],
                                                   rstd[:, which, t:t + 1], ALU.subtract, ALU.mult)
                last.then_inc(norm_ready, 1)

            def split_q(b):
                dve.wait_ge(qk_copied, b + 1)
                nc.vector.tensor_tensor(q_lo[:, span(b)], q_f[0:C, span(b)], q_hi[0:C, span(b)].bitcast(F32),
                                        ALU.subtract).then_inc(q_lo_ready, 1)

            def reduce_max(b, s):
                t, _, w, place = SLOTS[b][s]
                dve.wait_ge(max_scores, SLOTS_BEFORE[b] + s + 1)
                nc.vector.tensor_reduce(pmax[:, FIRST_TILE[b] + t, place:place + 1], MPAIR[:, s % 2, 0:w], AX.X,
                                        ALU.max).then_inc(max_reduced, 1)

            def finish_max(b):
                dve.wait_ge(max_reduced, SLOTS_BEFORE[b] + len(SLOTS[b]))
                nc.vector.tensor_reduce(nmax[:, tiles(b)], pmax[:, tiles(b), :], AX.X, ALU.max,
                                        negate=True).then_inc(nmax_ready, 1)

            def row_max(b):
                dve.wait_ge(max_row, b + 1)
                nc.vector.tensor_tensor(q_hi[C:CA, span(b)], MPAIR[C:CA, 0, 0:width(b)], q_f[C:CA, span(b)],
                                        ALU.add).then_inc(row_ready, 1)

            nc.vector.memset(flat(SPAIR[0])[C:CA, :], 1.0)
            nc.vector.memset(flat(SPAIR[1])[C:CA, :], 1.0).then_inc(psum_ones, 1)
            dve.wait_ge(x_in, 16)
            statistics(0, 0)
            normalize(0, 0)
            dve.wait_ge(x_later_in, 16)
            for b in range(1, NB):
                statistics(0, b)
            normalize(0, 1)
            for s in range(len(SLOTS[0])):
                reduce_max(0, s)
                if s == 3:
                    normalize(0, 2)
                    split_q(0)
            finish_max(0)
            row_max(0)
            for b in range(1, NB):
                split_q(b)

            def post(b, i):
                n, ts = width(b), tiles(b)
                nt = BLOCK_TILES[b]
                bank = UB[b % 2]
                proj = bank[:, 0:nt * (HID + 1)].rearrange("p (t h) -> p t h", h=HID + 1)
                if step_at(b, i, "gate"):
                    dve.wait_ge(projected, b + 1)
                    step(nc.vector.reciprocal(rsum[:, ts], proj[:, :, HID]))
                    dve.wait_ge(tanh_ready, 1)
                    step(nc.vector.tensor_scalar(gsum[:, ts], rsum[:, ts], tanh_g[:, 0:1], None, ALU.mult))
                if step_at(b, i, "residual"):
                    for t in range(nt):
                        ft = FIRST_TILE[b] + t
                        last = nc.vector.scalar_tensor_tensor(out=tok[:, ft, :], in0=proj[:, t, 0:HID],
                                                              scalar=gsum[:, ft:ft + 1], in1=tok[:, ft, :],
                                                              op0=ALU.mult, op1=ALU.add)
                    step(last)
                if step_at(b, i, "stats"):
                    statistics(1, b)
                if step_at(b, i, "normalize"):
                    normalize(1, b)
                if step_at(b, i, "split"):
                    dve.wait_ge(x_copied, NB + b + 1)
                    nc.vector.tensor_tensor(xT_lo[:, span(b)], xT[:, span(b)], xT_hi[:, span(b)].bitcast(F32),
                                            ALU.subtract).then_inc(xT_lo_ready, 1)
                if step_at(b, i, "shift"):
                    dve.wait_ge(logits_ready, b + 1)
                    dve.wait_ge(w_consts_in, 8 * 16)
                    step(nc.vector.tensor_tensor(lg[:, ts, :], bank[:, 0:nt * E].rearrange("p (t e) -> p t e", e=E),
                                                 br_sb[:, :].unsqueeze(1).to_broadcast([P, nt, E]), ALU.add))
                    step(nc.vector.tensor_reduce(lmax[:, ts], lg[:, ts, :], AX.X, ALU.max))
                    nc.vector.tensor_tensor(ld[:, ts, :], lg[:, ts, :],
                                            lmax[:, ts].unsqueeze(2).to_broadcast([P, nt, E]),
                                            ALU.subtract).then_inc(soft_in, 1)
                if step_at(b, i, "compare"):
                    own = lg[:, ts, :].unsqueeze(3).to_broadcast([P, nt, E, E])
                    other = lg[:, ts, :].unsqueeze(2).to_broadcast([P, nt, E, E])
                    nc.vector.tensor_tensor(cmp_gt[:, 0:nt, :, :], other, own, ALU.is_gt)
                    step(nc.vector.tensor_tensor(cmp_eq[:, 0:nt, :, :], other, own, ALU.is_equal))
                if step_at(b, i, "rank"):
                    dve.wait_ge(earlier_ready, 1)
                    step(nc.vector.tensor_tensor(cmp_eq[:, 0:nt, :, :], cmp_eq[:, 0:nt, :, :],
                                                 earlier[:, :, :].unsqueeze(1).to_broadcast([P, nt, E, E]),
                                                 ALU.mult))
                    step(nc.vector.tensor_tensor(cmp_gt[:, 0:nt, :, :], cmp_gt[:, 0:nt, :, :],
                                                 cmp_eq[:, 0:nt, :, :], ALU.add))
                    nc.vector.tensor_reduce(rank[:, ts, :], cmp_gt[:, 0:nt, :, :], AX.X, ALU.add)
                if step_at(b, i, "weights"):
                    dve.wait_ge(exp_ready, b + 1)
                    step(nc.vector.tensor_reduce(esum[:, ts], le[:, ts, :], AX.X, ALU.add))
                    step(nc.vector.reciprocal(einv[:, ts], esum[:, ts]))
                    step(nc.vector.tensor_tensor(le[:, ts, :], le[:, ts, :],
                                                 einv[:, ts].unsqueeze(2).to_broadcast([P, nt, E]), ALU.mult))
                if step_at(b, i, "pick"):
                    step(nc.vector.scalar_tensor_tensor(out=picked[:, ts, :], in0=rank[:, ts, :], scalar=2.0,
                                                        in1=le[:, ts, :], op0=ALU.is_lt, op1=ALU.mult))
                    step(nc.vector.tensor_reduce(psumw[:, ts], picked[:, ts, :], AX.X, ALU.add))
                    step(nc.vector.reciprocal(pinv[:, ts], psumw[:, ts]))
                if step_at(b, i, "share"):
                    nc.vector.tensor_tensor(routed[:, ts, :], picked[:, ts, :],
                                            pinv[:, ts].unsqueeze(2).to_broadcast([P, nt, E]),
                                            ALU.mult).then_inc(routed_ready, 1)

            def round_weights(e):
                dve.wait_ge(ex_used, (NB - 1) * UNITS + split_unit(e) + 1)
                dve.wait_ge(w_in[e % W_RING], 32 * (e // W_RING + 1))
                nc.vector.tensor_copy(w1_hi[:, e * H:(e + 1) * H], w_raw[:, e % W_RING, 0, :])
                nc.vector.tensor_copy(w2_hi[:, e, :, :].rearrange("p c d -> p (c d)"),
                                      w_raw[:, e % W_RING, 1, :]).then_inc(w_hi_ready, 1)

            for b in range(NB):
                n = width(b)
                for i in range(UNITS):
                    u = b * UNITS + i
                    js = unit_chunks(i)
                    for s in slots_at(b, i):
                        reduce_max(b + 1, s)
                    if b + 1 < NB and i == MAX_ROW_UNIT:
                        row_max(b + 1)
                    dve.wait_ge(ex_ready, u + 1)
                    if u >= P_RING:
                        dve.wait_ge(ex_used, u - P_RING + 1)
                    m = len(js) * n
                    nc.vector.tensor_tensor(ex_lo[:, u % P_RING, 0:m], ex[:, u % P_RING, 0:m],
                                            ex_hi[:, u % P_RING, 0:m].bitcast(F32), ALU.subtract).then_inc(lo_ready, 1)
                    for e in range(E):
                        if b == NB - 1 and i == min(split_unit(e) + LAG + 2, UNITS - 1):
                            round_weights(e)
                    if b + 1 < NB and i == MAX_ROW_UNIT - 2:
                        finish_max(b + 1)
                    if b:
                        post(b - 1, i)

            def scale_output(k, e, part=0, parts=1):
                w = SPAN // parts
                cut = slice(part * w, (part + 1) * w)
                if part == 0:
                    dve.wait_ge(h_used, k * FU + (e + 1) * HC)
                    dve.wait_ge(r_b_in[e % 2], 16 * (k * E // 2 + e // 2 + 1))
                    if k * (E - 1) + e > 2 and e:
                        dve.wait_ge(y_added, k * (E - 1) + max(e - 2, 0))
                dst = y_r[:, e % 2, cut] if e else acc[:, half(k)]
                nc.vector.scalar_tensor_tensor(out=dst, in0=MPAIR[:, e % 2, cut],
                                               scalar=cols[:, E * HC + e:E * HC + e + 1],
                                               in1=r_b[:, e % 2, cut], op0=ALU.add, op1=ALU.mult).then_inc(y_scaled, 1)

            def finish_span(k):
                dve.wait_ge(y_turned, k + 1)
                src = UB[0][:, 0:SPAN].rearrange("p (t d) -> p t d", d=P)
                nc.vector.scalar_tensor_tensor(out=result[:, half_tiles(k), :], in0=src, scalar=tanh_g[:, 1:2],
                                               in1=tok[:, half_tiles(k), :], op0=ALU.mult, op1=ALU.add).then_inc(result_ready, 1)

            for k in range(SPANS):
                for i in range(FU):
                    u = k * FU + i
                    e = i // HC
                    if u == SPANS * FU - 1:
                        scale_output(k, e - 1)
                    dve.wait_ge(h_ready, u + 1)
                    if u >= H_RING:
                        dve.wait_ge(h_used, u - H_RING + 1)
                    nc.vector.tensor_tensor(hid(ex_lo, u), hid(ex, u), hid(ex_hi, u).bitcast(F32),
                                            ALU.subtract).then_inc(h_lo_ready, 1)
                    if i % HC == H_LAG and e > 0 and u < SPANS * FU - 1:
                        scale_output(k, e - 1)
                    if i == H_LAG and k > 0:
                        scale_output(k - 1, E - 1)
                    if i == TURN_UNIT and k > 0:
                        finish_span(k - 1)
                    if k == 0:
                        post(NB - 1, u)
            for piece, base in enumerate((tok, result)):
                dve.wait_ge(sum_turned, piece + 1)
                src = UB[1 - piece][:, 0:SPAN].rearrange("p (t d) -> p t d", d=P)
                ts = half_tiles(SPANS - 1)
                step(nc.vector.scalar_tensor_tensor(out=result[:, ts, :], in0=src, scalar=tanh_g[:, 1:2],
                                                    in1=base[:, ts, :], op0=ALU.mult, op1=ALU.add))
            for part in range(END_PARTS):
                scale_output(SPANS - 1, E - 1, part, END_PARTS)
            for part in range(END_PARTS):
                dve.wait_ge(y_turned, SPANS + part)
                src = ps[:, part, 0:SPAN // END_PARTS].rearrange("p (t d) -> p t d", d=P)
                ts = last_tiles(part)
                nc.vector.scalar_tensor_tensor(out=result[:, ts, :], in0=src, scalar=tanh_g[:, 1:2],
                                               in1=result[:, ts, :], op0=ALU.mult, op1=ALU.add).then_inc(result_ready, 1)

        @block.tensor
        def _(pe):
            pe.wait_ge(ident_ready, 1)
            for _ in range(WARM_UP):
                nc.tensor.transpose(MPAIR[:, 0, 0:P], ident[:, :], ident[:, :])
            pe.wait_ge(small_in, 4 * 16)
            nc.tensor.transpose(UB[1][:, 0:CA], wk_sb[:, :], ident[0:CA, 0:CA]).then_inc(small_turned, 1)

            def turn_ctx(g, start, end):
                js = group_chunks(g)
                if start == 0:
                    pe.wait_ge(ctx_in[g], 16 if js[-1] < FULL else 32)
                    if g >= 2:
                        pe.wait_ge(ctxT_f_ready, g - 1)
                for k in range(start, min(end, len(js))):
                    ins = nc.tensor.transpose(flat(SPAIR[g % 2])[0:C, k * P:(k + 1) * P], raw[:, js[k], :], ident[:, :])
                    if k == len(js) - 1:
                        ins.then_inc(ctx_turned, 1)

            def turn_x(which, b, bank):
                pe.wait_ge(norm_ready, which * NB + b + 1)
                for t in range(BLOCK_TILES[b]):
                    last = nc.tensor.transpose(bank[:, t * P:(t + 1) * P], norm[:, FIRST_TILE[b] + t, :], ident[:, :])
                last.then_inc(x_turned, 1)

            def make_q(b):
                pe.wait_ge(small_copied, 1)
                pe.wait_ge(x_copied, b + 1)
                nc.tensor.matmul(UB[1][:, 0:width(b)], wq_sb[:, :], xT[:, span(b)], start=True, stop=True).then_inc(q_made, 1)

            def make_qk(b):
                pe.wait_ge(q_copied, b + 1)
                nc.tensor.matmul(UB[0][0:CA, 0:width(b)], wkT[:, :], qT[:, 0:width(b)], start=True,
                                 stop=True).then_inc(qk_made, 1)

            def score_for_max(b, s):
                t, key, w, place = SLOTS[b][s]
                ft = FIRST_TILE[b] + t
                if s >= 2:
                    pe.wait_ge(max_reduced, SLOTS_BEFORE[b] + s - 1)
                elif b:
                    pe.wait_ge(row_ready, b)
                nc.tensor.matmul(MPAIR[:, s % 2, 0:w], q_hi[:, ft * P:(ft + 1) * P], ctxT_hi[0:CA, key:key + w],
                                 start=True, stop=True).then_inc(max_scores, 1)

            def turn_max(b):
                pe.wait_ge(nmax_ready, b + 1)
                for t in range(BLOCK_TILES[b]):
                    ft = FIRST_TILE[b] + t
                    last = nc.tensor.matmul(MPAIR[C:CA, 0, t * P:(t + 1) * P], nmax[:, ft:ft + 1], ident[:, :],
                                            start=True, stop=True)
                last.then_inc(max_row, 1)

            turn_x(0, 0, UB[0])
            turn_ctx(0, 0, 3)
            make_q(0)
            turn_ctx(0, 3, TRANSPOSE_GROUP)
            make_qk(0)
            turn_ctx(1, 0, TRANSPOSE_GROUP)
            pe.wait_ge(q_hi_ready, 1)
            per_group = TRANSPOSE_GROUP * P // BANK * BLOCK_TILES[0]
            TURNED = [0, 0, 0, 4, TRANSPOSE_GROUP]
            assert per_group == len(TURNED) - 1

            def query_steps(g):
                for b in range(1, NB):
                    if Q_STEPS[b, "turn"] == g:
                        pe.wait_ge(qk_copied, b)
                        turn_x(0, b, UB[0])
                    if Q_STEPS[b, "q"] == g:
                        make_q(b)
                    if Q_STEPS[b, "qk"] == g:
                        make_qk(b)

            for g in range(NG):
                pe.wait_ge(ctxT_hi_ready, g + 1)
                if g == NG - 1:
                    pe.wait_ge(ones_ready, 1)
                for s in range(g * per_group, min((g + 1) * per_group, len(SLOTS[0]))):
                    score_for_max(0, s)
                    part = s - g * per_group
                    if part == 1:
                        query_steps(g)
                    if g + 2 < NG:
                        turn_ctx(g + 2, TURNED[part], TURNED[part + 1])
            pe.wait_ge(w_consts_in, 8 * 16)
            pe.wait_ge(qk_copied, NB)
            nc.tensor.transpose(UB[1][:, 0:NROW], rows[:, :], ident[0:NROW, 0:NROW]).then_inc(rows_turned, 1)
            turn_max(0)

            def scores(b, i):
                u = b * UNITS + i
                n = width(b)
                if i == 0:
                    pe.wait_ge(row_ready, b + 1)
                    pe.wait_ge(q_lo_ready, b + 1)
                if b == 0:
                    pe.wait_ge(ctxT_lo_ready, unit_chunks(i)[-1] // TRANSPOSE_GROUP + 1)
                if u < 2:
                    pe.wait_ge(ctxT_f_ready, NG)
                if u >= 2:
                    pe.wait_ge(ex_ready, u - 1)
                for k, j in enumerate(unit_chunks(i)):
                    dst = SPAIR[u % 2][:, k, 0:n]
                    keys = slice(j * P, (j + 1) * P)
                    nc.tensor.matmul(dst, ctxT_hi[0:CA, keys], q_hi[:, span(b)], start=True, stop=False)
                    nc.tensor.matmul(dst, ctxT_hi[0:C, keys], q_lo[:, span(b)], start=False, stop=False)
                    last = nc.tensor.matmul(dst, ctxT_lo[0:C, keys], q_hi[0:C, span(b)], start=False, stop=True)
                last.then_inc(scores_ready, 1)

            def values(b, i):
                u = b * UNITS + i
                n = width(b)
                js = unit_chunks(i)
                dst = UB[b % 2]
                pe.wait_ge(lo_ready, u + 1)
                if b == 0:
                    g = js[-1] // TRANSPOSE_GROUP
                    pe.wait_ge(ctx_lo_ready, g + 1)
                if i == 0 and b >= 2:
                    pe.wait_ge(r_copied, b - 1)
                if i == 0 and b == 1:
                    pe.wait_ge(rows_copied, 1)
                for k, j in enumerate(js):
                    hi = ex_hi[:, u % P_RING, k * n:(k + 1) * n]
                    lo = ex_lo[:, u % P_RING, k * n:(k + 1) * n]
                    nc.tensor.matmul(dst[0:CA, 0:n], ch[:, j, :], hi, start=(j == 0), stop=False)
                    nc.tensor.matmul(dst[0:C, 0:n], cl[:, j, :], hi, start=False, stop=False)
                    last = nc.tensor.matmul(dst[0:CA, 0:n], ch[:, j, :], lo, start=False, stop=(j == NC - 1))
                last.then_inc(ex_used, 1)

            def post(b, i):
                n, nt = width(b), BLOCK_TILES[b]
                bank = UB[b % 2]
                if step_at(b, i, "project"):
                    pe.wait_ge(u_copied, b + 1)
                    pe.wait_ge(column_ready, 1)
                    for t in range(nt):
                        last = nc.tensor.matmul(bank[:, t * (HID + 1):(t + 1) * (HID + 1)], u_sb[:, t * P:(t + 1) * P],
                                                wv_sb[:, :], start=True, stop=True)
                    last.then_inc(projected, 1)
                if step_at(b, i, "turn"):
                    turn_x(1, b, bank)
                if step_at(b, i, "logits"):
                    pe.wait_ge(x_copied, NB + b + 1)
                    for t in range(nt):
                        ft = FIRST_TILE[b] + t
                        last = nc.tensor.matmul(bank[:, t * E:(t + 1) * E], xT[:, ft * P:(ft + 1) * P], wr_sb[:, :],
                                                start=True, stop=True)
                    last.then_inc(logits_ready, 1)
                if step_at(b, i, "turn_r"):
                    pe.wait_ge(routed_ready, b + 1)
                    for t in range(nt):
                        last = nc.tensor.transpose(bank[0:E, t * P:(t + 1) * P], routed[:, FIRST_TILE[b] + t, :],
                                                   ident[:, :])
                    last.then_inc(r_turned, 1)

            def hidden(k, i):
                u = k * FU + i
                if k == 0 and i % HC == 0:
                    pe.wait_ge(w_lo_ready, i // HC + 1)
                if i == 0:
                    pe.wait_ge(xT_lo_ready, BLOCKS_FOR[k])
                if u < EARLY_HIDDEN:
                    pe.wait_ge(ex_ready, NB * UNITS - 1)
                elif u < 4:
                    pe.wait_ge(ex_ready, NB * UNITS)
                if u >= 4:
                    pe.wait_ge(h_ready, u - 3)
                dst = bank_of_hidden(u)[:, 0:SPAN]
                rows_ = slice(i * P, (i + 1) * P)
                nc.tensor.matmul(dst, w1_hi[:, rows_], xT_hi[:, half(k)], start=True, stop=False)
                nc.tensor.matmul(dst, w1_hi[:, rows_], xT_lo[:, half(k)], start=False, stop=False)
                nc.tensor.matmul(dst, w1_lo[:, rows_], xT_hi[:, half(k)], start=False, stop=True).then_inc(h_made, 1)

            for v in range(NB * UNITS + LAG):
                b, i = divmod(v, UNITS)
                if b == NB:
                    hidden(0, i)
                if b < NB:
                    scores(b, i)
                    for s in slots_at(b, i):
                        score_for_max(b + 1, s)
                    if b + 1 < NB and i == MAX_ROW_UNIT:
                        turn_max(b + 1)
                    if b:
                        post(b - 1, i)
                if v >= LAG:
                    values(*divmod(v - LAG, UNITS))

            def expert_out(k, i):
                u = k * FU + i
                e, c = divmod(i, HC)
                pe.wait_ge(h_lo_ready, u + 1)
                if c == 0 and k * E + e >= 2:
                    pe.wait_ge(y_scaled, k * E + e - 1)
                dst = MPAIR[:, e % 2, 0:SPAN]
                hi, lo = hid(ex_hi, u), hid(ex_lo, u)
                nc.tensor.matmul(dst, w2_hi[:, e, c, :], hi, start=(c == 0), stop=False)
                nc.tensor.matmul(dst, w2_hi[:, e, c, :], lo, start=False, stop=False)
                nc.tensor.matmul(dst, w2_lo[:, e, c, :], hi, start=False, stop=(c == HC - 1)).then_inc(h_used, 1)

            def turn_sum(k, experts, bank):
                pe.wait_ge(y_added, k * (E - 1) + experts - 1)
                for t in range(SPAN_TILES):
                    ft = k * SPAN_TILES + t
                    last = nc.tensor.transpose(bank[:, t * P:(t + 1) * P], acc[:, ft * P:(ft + 1) * P], ident[:, :])
                last.then_inc(y_turned if experts == E else sum_turned, 1)

            def turn_expert(e, tiles_, bank, done):
                for t in tiles_:
                    at = (t - tiles_[0]) * P
                    last = nc.tensor.transpose(bank[:, at:at + P], y_r[:, e % 2, t * P:(t + 1) * P], ident[:, :])
                last.then_inc(done, 1)

            for v in range(SPANS * FU + H_LAG):
                k, i = divmod(v, FU)
                if k < SPANS:
                    if v >= EARLY_HIDDEN:
                        hidden(k, i)
                    if k == 0:
                        post(NB - 1, i)
                    if k > 0 and i == TURN_UNIT:
                        turn_sum(k - 1, E, UB[0])
                if v == SPANS * FU - 1:
                    turn_sum(SPANS - 1, E - 2, UB[1])
                if v == SPANS * FU + H_LAG - 1:
                    pe.wait_ge(y_scaled, SPANS * E - 1)
                    pe.wait_ge(result_ready, SPANS - 1)
                    turn_expert(E - 2, range(SPAN_TILES), UB[0], sum_turned)
                if v >= H_LAG:
                    expert_out(*divmod(v - H_LAG, FU))
            for part in range(END_PARTS):
                pe.wait_ge(y_scaled, SPANS * E + part)
                turn_expert(E - 1, range(part * END_TILES, (part + 1) * END_TILES), ps[:, part, :], y_turned)


_INS = ['x', 'ctx_768', 'g_xattn', 'g_ffn', 'L0_xattn_Wq', 'L0_xattn_bq', 'L0_xattn_Wk', 'L0_xattn_bk',
        'L0_xattn_Wv', 'L0_xattn_bv', 'L0_ffn_W1', 'L0_ffn_b1', 'L0_ffn_W2', 'L0_ffn_b2', 'L0_ffn_Wr',
        'L0_ffn_br']
_OUTS = [((1, 1024, 128), 'float32')]


def kernel(**inputs):
    import numpy as _np
    import concourse.bacc as _bacc
    from concourse import mybir as _mybir
    from concourse.bass_utils import run_bass_kernel_spmd as _run

    nc = _bacc.Bacc("TRN2", target_bir_lowering=False, num_devices=1)
    arrays, args = {}, []
    for name in _INS:
        a = _np.ascontiguousarray(inputs[name])
        arrays[f"in_{name}_dram"] = a
        args.append(nc.dram_tensor(f"in_{name}_dram", a.shape, _mybir.dt.from_np(a.dtype), kind="ExternalInput").ap())
    for i, (shape, dtype) in enumerate(_OUTS):
        dt = _mybir.dt.from_np(_np.dtype(dtype))
        args.append(nc.dram_tensor(f"out_{i}_dram", shape, dt, kind="ExternalOutput").ap())
    attention_experts(nc, *args)
    r = _run(nc, [arrays], core_ids=[0])
    got = tuple(r.results[0][f"out_{i}_dram"] for i in range(len(_OUTS)))
    return got[0]
```
